# Optimizing a Trainium2 kernel written in Bass

```python
import numpy as np
import jax
import jax.numpy as jnp

def _softmax(x, axis=-1):
    return jax.nn.softmax(x, axis=axis)

def _gelu(x):
    return jax.nn.gelu(x, approximate=True)

def _silu(x):
    return jax.nn.silu(x)

def _sigmoid(x):
    return jax.nn.sigmoid(x)

def _layernorm(x, axis=-1, eps=1e-05):
    m = jnp.mean(x, axis=axis, keepdims=True)
    v = jnp.var(x, axis=axis, keepdims=True)
    return (x - m) / jnp.sqrt(v + eps)

def _scatter_add(tgt, idx, src, axis=0):
    return tgt.at[idx].add(src)

def _segment_sum(src, seg, n):
    return jax.ops.segment_sum(src, seg, n)
kernel_name = 'mk_decoder_preln_d1_seqx_r4_c623cf'

def setup_inputs(seed: int=0):
    np.random.seed(seed)
    _w = jnp.asarray

    def _rec_inputs():
        import jax
        import jax.numpy as jnp
        _rk = jax.random.key(seed)
        x = -0.0002928 + 1 * jax.random.normal(jax.random.fold_in(_rk, 1), (2, 1024, 256), jnp.float32)
        _lenS = 1024 - jax.random.randint(jax.random.fold_in(_rk, 7), (2,), 0, max(1, 1024 // 4) + 1, jnp.int32)
        _lenS2 = 64 - jax.random.randint(jax.random.fold_in(_rk, 8), (2,), 0, max(1, 64 // 4) + 1, jnp.int32)
        _ctx_768P = jax.random.normal(jax.random.fold_in(_rk, 11), (2, 16, 192), jnp.float32)
        _ctx_768c = jax.random.dirichlet(jax.random.fold_in(_rk, 511), 0.3 * jnp.ones((16,), jnp.float32), (2, 64))
        _ctx_768t = jnp.einsum('bsk,bkd->bsd', _ctx_768c, _ctx_768P)
        _ctx_768t = _ctx_768t * jax.lax.rsqrt(jnp.mean(jnp.square(_ctx_768t)) + 1e-12) * 0.953939
        ctx_768 = 2.09791e-05 + 1.00001 * (_ctx_768t + 0.3 * jax.random.normal(jax.random.fold_in(_rk, 611), (2, 64, 192), jnp.float32))
        return (x, ctx_768)
    x, ctx_768 = _rec_inputs()

    def _L0_attn_setup():
        import jax, jax.numpy as jnp
        import numpy as np
        DIM = 256
        HEADS = 16
        HEAD_DIM = DIM // HEADS
        NUM_FILTERS = 4
        NUM_TAPS = 101
        RES = 128

        def _fir_fft(c, sig):
            R = sig.shape[0]
            L = R + c.shape[0] - 1
            out = jnp.fft.ifft(jnp.fft.fft(sig, n=L) * jnp.fft.fft(c, n=L)).real
            return out[:R]
        key = jax.random.key(seed)
        ks = jax.random.split(key, 5)
        B, S = (2, 512)
        x = jax.random.normal(ks[0], (B, S, DIM), dtype=jnp.float32)
        Wqkv = jax.random.normal(ks[1], (3 * DIM, DIM), dtype=jnp.float32) * DIM ** (-0.5)
        Wout = jax.random.normal(ks[2], (DIM, DIM), dtype=jnp.float32) * DIM ** (-0.5)
        Wpos = jax.random.normal(ks[3], (HEADS, NUM_FILTERS), dtype=jnp.float32) * 0.5
        coeffs = jax.random.normal(ks[4], (NUM_FILTERS, NUM_TAPS), dtype=jnp.float32) * 0.05
        return {'x': x, 'Wqkv': Wqkv, 'Wout': Wout, 'Wpos': Wpos, 'coeffs': coeffs}
    _L0_attn_all = _L0_attn_setup()
    _L0_attn_in = {k: v for k, v in _L0_attn_all.items() if k in ('Wqkv', 'Wout', 'Wpos', 'coeffs')}
    del _L0_attn_all

    def _L0_xattn_setup():
        import jax, jax.numpy as jnp
        import numpy as np
        N_HEADS = 16
        D_HEAD = 64
        key = jax.random.key(seed)
        ks = jax.random.split(key, 7)
        B, SQ, SKV = (2, 512, 512)
        D_MODEL, D_COND, D_ATTN = (256, 192, N_HEADS * D_HEAD)
        return {'x': jax.random.normal(ks[0], (B, SQ, D_MODEL), jnp.float32), 'cond': jax.random.normal(ks[1], (B, SKV, D_COND), jnp.float32), 'w_q': jax.random.normal(ks[2], (D_MODEL, D_ATTN), jnp.float32) * D_MODEL ** (-0.5), 'w_k': jax.random.normal(ks[3], (D_COND, D_ATTN), jnp.float32) * D_COND ** (-0.5), 'w_v': jax.random.normal(ks[4], (D_COND, D_ATTN), jnp.float32) * D_COND ** (-0.5), 'w_out': jax.random.normal(ks[5], (D_ATTN, D_MODEL), jnp.float32) * D_ATTN ** (-0.5), 'b_out': jnp.zeros((D_MODEL,), jnp.float32)}
    _L0_xattn_all = _L0_xattn_setup()
    _L0_xattn_in = {k: v for k, v in _L0_xattn_all.items() if k in ('w_q', 'w_k', 'w_v', 'w_out', 'b_out')}
    del _L0_xattn_all

    def _L0_ffn_setup():
        import jax, jax.numpy as jnp
        import numpy as np
        TOPK = 2
        CAPACITY_FACTOR = 1.0
        EPS = 1e-06
        B, S, D = (4, 1024, 256)
        E = 8
        SUB_H = 512 // E
        key = jax.random.key(seed)
        ks = jax.random.split(key, 7)
        x = jax.random.normal(ks[0], (B, S, D), dtype=jnp.float32)
        w_gate_w = jax.random.normal(ks[1], (D, E), dtype=jnp.float32) * 0.02
        w_gate_b = jnp.zeros((E,), jnp.float32)
        W1 = jax.random.normal(ks[2], (E, D, SUB_H), dtype=jnp.float32) * 0.02
        b1 = jnp.zeros((E, SUB_H), jnp.float32)
        W2 = jax.random.normal(ks[3], (E, SUB_H, D), dtype=jnp.float32) * 0.02
        b2 = jnp.zeros((E, D), jnp.float32)
        return {'x': x, 'w_gate_w': w_gate_w, 'w_gate_b': w_gate_b, 'W1': W1, 'b1': b1, 'W2': W2, 'b2': b2}
    _L0_ffn_all = _L0_ffn_setup()
    _L0_ffn_in = {k: v for k, v in _L0_ffn_all.items() if k in ('w_gate_w', 'w_gate_b', 'W1', 'b1', 'W2', 'b2')}
    del _L0_ffn_all
    return {'x': x, 'ctx_768': ctx_768, 'L0_attn_Wqkv': _L0_attn_in['Wqkv'], 'L0_attn_Wout': _L0_attn_in['Wout'], 'L0_attn_Wpos': _L0_attn_in['Wpos'], 'L0_attn_coeffs': _L0_attn_in['coeffs'], 'L0_xattn_w_q': _L0_xattn_in['w_q'], 'L0_xattn_w_k': _L0_xattn_in['w_k'], 'L0_xattn_w_v': _L0_xattn_in['w_v'], 'L0_xattn_w_out': _L0_xattn_in['w_out'], 'L0_xattn_b_out': _L0_xattn_in['b_out'], 'L0_ffn_w_gate_w': _L0_ffn_in['w_gate_w'], 'L0_ffn_w_gate_b': _L0_ffn_in['w_gate_b'], 'L0_ffn_W1': _L0_ffn_in['W1'], 'L0_ffn_b1': _L0_ffn_in['b1'], 'L0_ffn_W2': _L0_ffn_in['W2'], 'L0_ffn_b2': _L0_ffn_in['b2']}

def reference(x, ctx_768, L0_attn_Wqkv, L0_attn_Wout, L0_attn_Wpos, L0_attn_coeffs, L0_xattn_w_q, L0_xattn_w_k, L0_xattn_w_v, L0_xattn_w_out, L0_xattn_b_out, L0_ffn_w_gate_w, L0_ffn_w_gate_b, L0_ffn_W1, L0_ffn_b1, L0_ffn_W2, L0_ffn_b2):
    import jax
    import jax.numpy as jnp

    def _L0_attn_ref(x, Wqkv, Wout, Wpos, coeffs):
        import jax, jax.numpy as jnp
        import numpy as np
        DIM = 256
        HEADS = 16
        HEAD_DIM = DIM // HEADS
        NUM_FILTERS = 4
        NUM_TAPS = 101
        RES = 128

        def _fir_fft(c, sig):
            R = sig.shape[0]
            L = R + c.shape[0] - 1
            out = jnp.fft.ifft(jnp.fft.fft(sig, n=L) * jnp.fft.fft(c, n=L)).real
            return out[:R]
        B, S, D = x.shape
        scale = HEAD_DIM ** (-0.5)
        proto = jnp.linspace(0.0, 1.0, RES).astype(x.dtype)
        table = jax.vmap(_fir_fft, in_axes=(0, None))(coeffs, proto).T
        r = jnp.arange(S)
        rel = jnp.abs(r[None, :] - r[:, None]).astype(jnp.float32) / max(S - 1, 1)
        idx = jnp.clip(jnp.round(rel * (RES - 1)).astype(jnp.int32), 0, RES - 1)
        pos_feat = table[idx]
        pos_bias = jnp.einsum('ijf,hf->hij', pos_feat, Wpos)
        qkv = jnp.einsum('bsd,ed->bse', x, Wqkv)
        q, k, v = jnp.split(qkv, 3, axis=-1)
        q = q.reshape(B, S, HEADS, HEAD_DIM)
        k = k.reshape(B, S, HEADS, HEAD_DIM)
        v = v.reshape(B, S, HEADS, HEAD_DIM)
        logits = jnp.einsum('bihd,bjhd->bhij', q, k) * scale + pos_bias[None]
        attn = jax.nn.softmax(logits, axis=-1)
        out = jnp.einsum('bhij,bjhd->bihd', attn, v).reshape(B, S, D)
        return jnp.einsum('bsd,ed->bse', out, Wout)

    def _L0_xattn_ref(x, cond, w_q, w_k, w_v, w_out, b_out):
        import jax, jax.numpy as jnp
        import numpy as np
        N_HEADS = 16
        D_HEAD = 64
        B, SQ, _ = x.shape
        SKV = cond.shape[1]
        scale = D_HEAD ** (-0.5)
        q = (x @ w_q).reshape(B, SQ, N_HEADS, D_HEAD)
        k = (cond @ w_k).reshape(B, SKV, N_HEADS, D_HEAD)
        v = (cond @ w_v).reshape(B, SKV, N_HEADS, D_HEAD)
        attn = jnp.einsum('bqhd,bkhd->bhqk', q, k) * scale
        attn = jax.nn.softmax(attn, axis=-1)
        out = jnp.einsum('bhqk,bkhd->bqhd', attn, v).reshape(B, SQ, N_HEADS * D_HEAD)
        return out @ w_out + b_out

    def _L0_ffn_ref(x, w_gate_w, w_gate_b, W1, b1, W2, b2):
        import jax, jax.numpy as jnp
        import numpy as np
        TOPK = 2
        CAPACITY_FACTOR = 1.0
        EPS = 1e-06
        B, S, D = (4, 1024, 256)
        E = 8
        SUB_H = 512 // E
        Bx, Sx, Dx = x.shape
        Ex = w_gate_b.shape[0]
        K = Sx // 2
        capacity = int(CAPACITY_FACTOR * Bx)
        gate_scores = jax.nn.softmax(x @ w_gate_w + w_gate_b, axis=-1)
        _, top_idx = jax.lax.top_k(gate_scores, TOPK)
        mask = jax.nn.one_hot(top_idx, Ex, dtype=gate_scores.dtype).sum(axis=-2)
        masked = gate_scores * mask
        denom = masked.sum(axis=0, keepdims=True) + EPS
        route = masked / denom * capacity
        route_eb = jnp.transpose(route, (2, 0, 1))
        _, seq_ids = jax.lax.top_k(route_eb, K)
        seq_ids = jnp.sort(seq_ids, axis=-1)
        xg = jax.vmap(lambda idx: jnp.take_along_axis(x, idx[..., None], axis=1))(seq_ids)
        h = jnp.einsum('ebkd,edh->ebkh', xg, W1) + b1[:, None, None, :]
        h = jax.nn.gelu(h, approximate=False)
        o = jnp.einsum('ebkh,ehd->ebkd', h, W2) + b2[:, None, None, :]
        flat_ids = (jnp.arange(Bx)[None, :, None] * Sx + seq_ids).reshape(-1)
        outs = jnp.zeros((Bx * Sx, Dx), x.dtype).at[flat_ids].add(o.reshape(-1, Dx))
        return outs.reshape(Bx, Sx, Dx)
    x = x + _L0_attn_ref(_layernorm(x, axis=-1), L0_attn_Wqkv, L0_attn_Wout, L0_attn_Wpos, L0_attn_coeffs)
    x = x + _L0_xattn_ref(_layernorm(x, axis=-1), ctx_768, L0_xattn_w_q, L0_xattn_w_k, L0_xattn_w_v, L0_xattn_w_out, L0_xattn_b_out)
    x = x + _L0_ffn_ref(_layernorm(x, axis=-1), L0_ffn_w_gate_w, L0_ffn_w_gate_b, L0_ffn_W1, L0_ffn_b1, L0_ffn_W2, L0_ffn_b2)
    return x

_drawn_inputs = setup_inputs


def setup_inputs(seed=0):
    import zlib

    import numpy as np

    out = dict(_drawn_inputs(seed))
    spreads = {'L0_xattn_b_out': (0.0, 0.1),
     'L0_ffn_w_gate_b': (0.0, 0.1),
     'L0_ffn_b1': (0.0, 0.55),
     'L0_ffn_b2': (0.0, 0.1)}
    factors = {'L0_attn_Wpos': 6.384, 'L0_attn_coeffs': 8.0}
    for name, (base, spread) in spreads.items():
        noise = np.random.default_rng([zlib.crc32(name.encode()), seed]).standard_normal(out[name].shape)
        drawn = base * np.exp(spread * noise) if base else spread * noise
        out[name] = jnp.asarray(drawn.astype(out[name].dtype))
    for name, factor in factors.items():
        out[name] = (out[name] * factor).astype(out[name].dtype)
    return out
```

```python
from contextlib import ExitStack

import concourse.bass as bass
from concourse import mybir

F32 = mybir.dt.float32
BF16 = mybir.dt.bfloat16
U32 = mybir.dt.uint32
I32 = mybir.dt.int32
ALU = mybir.AluOpType
ACT = mybir.ActivationFunctionType
AX = mybir.AxisListType

P = 128
B, S, D = 2, 1024, 256
TPB = S // P
NT = B * TPB
TOK = B * S
CC = D // P
H, DH = 16, 16
SCALE = DH ** -0.5
RES, TAPS, NF = 128, 101, 4
LINE = 2 * S
SLAB = S + (TPB - 1) * P
XH, XD = 16, 64
KV, DC = 64, 192
XSCALE = XD ** -0.5
HKV = XH * KV
NK = XH * XD // P
E, SUB = 8, 64
NM = E * SUB // P
TOPK, KSEL = 2, S // 2
LN_EPS, DEN_EPS = 1e-5, 1e-6

STACK = 6 * DH + 2
SHIFT_ROW = 6 * DH
AHEAD = 6
RING = 4
UNITS = 4
STEPS = H // 2
TILES = UNITS * TPB
BANKS = 8
UMARGIN = 1.05

Q_ROWS = {1: [(0, 1, 1), (4, 2, 1)], 2: [(1, 2, 2)], 3: [(2, 1, 1)]}
K_ROWS = {1: [(0, 3, 1)], 2: [(3, 2, 1)], 3: [(5, 1, 1)]}


class Counter:

    def __init__(self, eng, sem):
        self.eng, self.sem, self.n = eng, sem, 0

    def __call__(self, ins):
        self.n += 1
        ins.then_inc(self.sem, 1)
        self.eng.wait_ge(self.sem, self.n)


def decoder_layer(nc, x, ctx_in, w_qkv, w_o, w_pos, coeffs, xw_q, xw_k, xw_v, xw_o, xb_o,
                  gate_w, gate_b, ffn_w1, ffn_b1, ffn_w2, ffn_b2, out):
    with ExitStack() as stack:
        def sb(name, shape, dt=F32):
            return stack.enter_context(nc.sbuf_tensor(name, shape, dt))

        def sem(name):
            return stack.enter_context(nc.semaphore(name))

        ps = stack.enter_context(nc.psum_tensor("ps", [P, BANKS, 512], F32))

        xt = sb("xt", [P, NT, D])
        xn = sb("xn", [P, 2, 4, D])
        lnT = sb("lnT", [P, CC, TOK])
        o_all = sb("o_all", [P, NT, (H + 1) * DH])
        lnTr = o_all[:, :, :].rearrange("p a b -> p (a b)")[:, 0:CC * TOK].rearrange("p (c t) -> p c t", c=CC)
        big = sb("big", [P, NT * H * 32])
        v_all = big[:, :].rearrange("p (t h d) -> p t h d", t=NT, h=H)
        hid = big[:, :].rearrange("p (m t) -> p m t", m=NM)
        ring = sb("ring", [P, RING, 2 * S])
        side = sb("side", [P, 7936])
        v_st = sb("v_st", [P, UNITS, TPB, 32])
        o_sb = sb("o_sb", [P, 2, D])
        wT = sb("wT", [P, CC, 3 * D])
        woT = sb("woT", [P, CC, D])
        xa = sb("xa", [P, CC, B, HKV])
        xvw = sb("xvw", [P, B, NK, D])
        ident = sb("ident", [P, P])
        anti = sb("anti", [P, P])
        ones = sb("ones", [P, P])
        bo_bc = sb("bo_bc", [P, D])
        eps = sb("eps", [P, 1])
        st = sb("st", [P, 4, 6])
        mv = sb("mv", [P, 4, 2])
        ln_s = sb("ln_s", [P, 5, 4])
        rs = sb("rs", [P, 2, 4])
        low = sb("low", [P, 2, 4])
        head_s = sb("head_s", [H, 8])
        x_s = sb("x_s", [P, 2, 4, XH])
        b1_sb = sb("b1_sb", [P, NM])
        gb_sb = sb("gb_sb", [E, 1])
        r_s = sb("r_s", [P, 16])

        def cut(region, at, shape, dt=F32):
            n = 1
            for s in shape[1:]:
                n *= s
            n = n * (2 if dt == BF16 else 4) // 4
            v = region[0:shape[0], at:at + n]
            if dt != F32:
                v = v.bitcast(dt)
            if len(shape) == 3:
                v = v.rearrange("p (a b) -> p a b", b=shape[2])
            if len(shape) == 4:
                v = v.rearrange("p (a b c) -> p a b c", b=shape[2], c=shape[3])
            return v, at + n

        ring_f = ring[:, :, :].rearrange("p a b -> p (a b)")
        xvw_f = xvw[:, :, :, :].rearrange("p a b c -> p (a b c)")
        onehot, at = cut(ring_f, 0, [P, LINE])
        parts, at = cut(ring_f, at, [P, 2, 3, TOK], BF16)
        w_nat, at = cut(xvw_f, 0, [P, 6, D])
        wo_nat, at = cut(xvw_f, at, [P, CC, D])
        wq_nat, at = cut(big, 0, [P, CC, XH * XD])
        wqT, at = cut(big, at, [P, NK, D])
        wk_nat, at = cut(big, at, [P, 2, XH * XD])
        wv_nat, at = cut(big, at, [P, 2, XH * XD])
        xwo, at = cut(side, 0, [P, NK, D])
        kbd, at = cut(side, at, [P, B * NK, P])
        vbd, at = cut(side, at, [P, B * NK, P])
        ctx_nat, at = cut(side, at, [P, DC])
        ctxT, at = cut(side, at, [P, 2, P])
        ramp, at = cut(side, at, [TAPS, RES])
        ceff, at = cut(side, at, [TAPS, H])
        biasT, at = cut(side, at, [RES, H])
        coef_sb, at = cut(side, at, [NF, TAPS])
        wposT, at = cut(side, at, [NF, H])
        norm_sel, at = cut(side, at, [P, 2, 32], BF16)
        v_st_f = v_st[:, :, :, :].rearrange("p a b c -> p (a b c)")
        o_sb_f = o_sb[:, :, :].rearrange("p a b -> p (a b)")
        sq, _ = cut(v_st_f, 0, [P, 4, 512], BF16)
        resid, _ = cut(xn[:, :, :, :].rearrange("p a b c -> p (a b c)"), 0, [P, 2, 512])
        line_sb, _ = cut(side, 0, [H, LINE])
        qn2, _ = cut(side, 2048, [H, TOK])
        shift, _ = cut(side, 4096, [H, TOK])
        shift_p, _ = cut(ring_f, 0, [H, 2, TOK], BF16)
        slab = side[:, 0:2 * SLAB].rearrange("p (a b) -> p a b", a=2)
        st_q = side[:, 2 * SLAB:2 * SLAB + 4 * 512].bitcast(BF16).rearrange("p (a b) -> p a b", a=UNITS)
        st_k = side[:, 2 * SLAB + 4 * 512:2 * SLAB + 8 * 512].bitcast(BF16).rearrange("p (a b) -> p a b", a=UNITS)
        xd, at = cut(ring_f, 0, [P, 2, HKV])
        xe, at = cut(ring_f, at, [P, 2, HKV])
        xp, at = cut(ring_f, at, [P, 2, HKV])
        xpT, at = cut(ring_f, at, [P, 2, HKV])
        w1, at = cut(side, 0, [P, CC, E * SUB])
        w2, at = cut(side, at, [P, NM, D])
        b2x, at = cut(side, at, [P, B, D])
        pick, at = cut(side, at, [P, B * NM, P], BF16)
        sel_b, at = cut(side, at, [P, S], BF16)
        block8, at = cut(side, at, [P, P], BF16)
        digits, at = cut(side, at, [P, 10], U32)
        gates, at = cut(side, at, [P, 4, NT * E])
        expw, at = cut(side, at, [P, E])
        sel_f, at = cut(side, at, [P, S])
        assert at <= 7936
        gT, at = cut(ring_f, 0, [E, TOK])
        rrep, at = cut(ring_f, at, [P, TPB, P])
        rr, at = cut(ring_f, at, [P, S])
        junk, at = cut(ring_f, at, [P, S])
        above, at = cut(ring_f, at, [P, S])
        prefix, at = cut(ring_f, at, [P, S])
        o_out, _ = cut(xn[:, :, :, :].rearrange("p a b c -> p (a b c)"), 0, [P, 4, 2 * D])

        d_q = nc.dram_tensor("d_q", (7, H * DH, TOK), BF16, kind="Internal").ap()
        d_k = nc.dram_tensor("d_k", (7, H * DH, TOK), BF16, kind="Internal").ap()
        d_line = nc.dram_tensor("d_line", (H, LINE), F32, kind="Internal").ap()

        small_in, x_in = sem("small_in"), [sem(f"x_in{g}") for g in range(4)]
        w_in, xw_in, xwo_in, ffn_in = sem("w_in"), sem("xw_in"), sem("xwo_in"), sem("ffn_in")
        const_step, const_ready = sem("const_step"), sem("const_ready")
        dve_step, act_step, pool_step = sem("dve_step"), sem("act_step"), sem("pool_step")
        job_done, act_took, dve_took = sem("job_done"), sem("act_took"), sem("dve_took")
        ln_var, ln_sd, ln_done = sem("ln_var"), sem("ln_sd"), sem("ln_done")
        part1_done, resid_done, part3_done = sem("part1_done"), sem("resid_done"), sem("part3_done")
        parts_out, line_out, shift_out = sem("parts_out"), sem("line_out"), sem("shift_out")
        line_done, bound_done, root_done, shift_done = sem("line_done"), sem("bound_done"), sem("root_done"), sem("shift_done")
        region_ready = sem("region_ready")
        stack_in = [sem(f"stack_in{u}") for u in range(UNITS)]
        slab_in = [sem(f"slab_in{h}") for h in range(2)]
        qk_done, add_done, exp_done, pv_done = sem("qk_done"), sem("add_done"), sem("exp_done"), sem("pv_done")
        heads_out, turned, finished, v_staged = sem("heads_out"), sem("turned"), sem("finished"), sem("v_staged")
        attn_step = sem("attn_step")
        bo_added, centred, xexp_done, xrecip_done, xprob_done = (
            sem("bo_added"), sem("centred"), sem("xexp_done"), sem("xrecip_done"), sem("xprob_done"))
        x2_done, rrep_done, digit_asked, chosen, out_done, stored = (
            sem("x2_done"), sem("rrep_done"), sem("digit_asked"), sem("chosen"), sem("out_done"),
            [sem(f"stored{i}") for i in range(4)])
        ffn_const, gate_in, v_zeroed, stage_go = sem("ffn_const"), sem("gate_in"), sem("v_zeroed"), sem("stage_go")
        gw_sb = sb("gw_sb", [P, CC, E])

        jobs = []
        jobs += [("wT", n, "act") for n in range(3)] + [("woT", 0, "act")]
        jobs += [("wqT", n, "act") for n in range(4)] + [("ctxT", 0, "act")]
        jobs += [("kT", n, "act") for n in range(2)] + [("vT", n, "dve") for n in range(2)]
        jobs += [("xa", n, "act") for n in range(8)] + [("xvw", n, "dve") for n in range(8)]
        jobs += [("ceff", 0, "dve"), ("biasT", 0, "dve")] + [("line", n, "dve") for n in range(4)]
        for g in range(4):
            jobs += [("lnT", (g, c), "act") for c in range(CC)] + [("lnTr", (g, c), "dve") for c in range(CC)]
        proj_order = [(half, n, e) for half in range(2) for n in range(4) for e in range(2)]
        for i, (half, n, e) in enumerate(proj_order):
            jobs.append(("proj", (half, n, e), "dve"))
            if e == 1 and i > 1:
                jobs.append(("norm", i // 2 - 1, "dve"))
        jobs.append(("norm", 7, "dve"))
        jobs += [("v", n, "act") for n in range(NT // 2)]
        jobs += [("oT", (g, c), "act") for g in range(4) for c in range(CC)]
        jobs += [("wo", n, "dve") for n in range(NT // 2)]
        jobs += [("ln2T", (g, c), "act") for g in range(4) for c in range(CC)]
        XLAG = 2
        for t in range(NT + XLAG):
            if t < NT:
                jobs += [("xl", (t, hf), "dve") for hf in range(2)]
            if t >= XLAG:
                jobs += [("xpT", (t - XLAG, hf), "act") for hf in range(2)] + [("xo", t - XLAG, "dve")]
        jobs += [("ln3T", (g, c), "act") for g in range(4) for c in range(CC)]
        jobs += [("gate", n, "act") for n in range(4)] + [("gateT", 0, "dve")]
        w1_order = [(m, n) for m in range(NM) for n in range(4)]
        jobs += [("w1", k, "act") for k in w1_order[:5]]
        jobs += [("rrep", n, "dve") for n in range(2)]
        for i in range(10):
            jobs += [("digit", i, "dve"), ("w1", w1_order[5 + i], "act")]
        jobs += [("w1", k, "act") for k in w1_order[15:]]
        jobs += [("mask", k, "dve") for k in w1_order]
        jobs += [("w2", t, "dve") for t in range(NT)]
        index = {(name, key): j for j, (name, key, _) in enumerate(jobs)}
        took = {"act": act_took, "dve": dve_took}

        def taken(eng, j):
            who = jobs[j][2]
            eng.wait_ge(took[who], sum(k[2] == who for k in jobs[:j + 1]))

        def bank(j):
            return ps[:, j % BANKS, :]

        def job(pe, name, key):
            j = index[name, key]
            if j >= BANKS:
                taken(pe, j - BANKS)
            return bank(j)

        def result(eng, name, key):
            j = index[name, key]
            eng.wait_ge(job_done, j + 1)
            return bank(j)

        def after(eng, name, key):
            eng.wait_ge(job_done, index[name, key] + 1)

        lnr_at = [(g // 2) * S + 512 * (1 - g % 2) for g in range(4)]

        ADD0, PV0, OUT0, TURN0, FIN0 = 4, 5, 1, 0, 1
        slot_of = [g % 3 for g in range(TILES)]
        before = {}
        for g in range(TILES):
            k = g - 1
            while slot_of[k % TILES] != slot_of[g]:
                k -= 1
            before[g] = g - k

        block = stack.enter_context(nc.Block())

        @block.sync
        def _(sp):
            sp.dma_start(w_nat, w_qkv.rearrange("(a p) c -> p a c", p=P)).then_inc(w_in, 16)
            sp.dma_start(wo_nat, w_o.rearrange("(a p) c -> p a c", p=P)).then_inc(w_in, 16)
            for g in range(4):
                sp.dma_start(xt[:, 4 * g:4 * g + 4, :],
                             x.rearrange("b (t p) c -> p (b t) c", p=P)[:, 4 * g:4 * g + 4, :]).then_inc(x_in[g], 16)
            sp.dma_start(wq_nat, xw_q.rearrange("(a p) n -> p a n", p=P)).then_inc(xw_in, 16)
            for w_sb, w in ((wk_nat, xw_k), (wv_nat, xw_v)):
                sp.dma_start(w_sb[:, 0, :], w[0:P, :]).then_inc(xw_in, 16)
                sp.dma_start(w_sb[0:DC - P, 1, :], w[P:DC, :]).then_inc(xw_in, 16)
            sp.dma_start(xwo, xw_o.rearrange("(k p) n -> p k n", p=P)).then_inc(xwo_in, 16)
            sp.wait_ge(line_done, 1)
            sp.dma_start(d_line, line_sb).then_inc(line_out, 16)
            for half, rows, dst in ((0, Q_ROWS, d_q), (1, K_ROWS, d_k)):
                sp.wait_ge(part3_done, 8 * (half + 1))
                for e in range(2):
                    for part, runs in rows.items():
                        for first, n, step in runs:
                            to = dst[first:first + step * (n - 1) + 1:step, e * P:(e + 1) * P, :].rearrange("r q t -> q r t")
                            frm = parts[:, e, part - 1, :].unsqueeze(1).broadcast_to([P, n, TOK])
                            sp.dma_start(to, frm).then_inc(parts_out, 16)
                sp.wait_ge(parts_out, 16 * (8 if half == 0 else 14))
                sp.sem_inc(region_ready, 1)
            sp.wait_ge(shift_done, 1)
            for k in range(2):
                sp.dma_start(d_q[6].rearrange("(h r) t -> h r t", r=DH)[:, k, :], shift_p[:, k, :]).then_inc(shift_out, 16)
            sp.wait_ge(shift_out, 32)
            sp.wait_ge(line_out, 16)
            sp.wait_ge(v_staged, UNITS)

            def load_stack(head, u):
                b = u % 2
                for dst, src in ((st_q, d_q), (st_k, d_k)):
                    v = bass.AP(tensor=src.tensor, offset=head * (DH * TOK) + b * S,
                                ap=[[H * DH * TOK, 6], [TOK, DH], [1, S]])
                    sp.dma_start(dst[0:SHIFT_ROW, u, :], v).then_inc(stack_in[u], 16)
                v = bass.AP(tensor=d_q.tensor, offset=6 * H * DH * TOK + head * (DH * TOK) + b * S,
                            ap=[[TOK, 2], [1, S]])
                sp.dma_start(st_q[SHIFT_ROW:STACK, u, :], v).then_inc(stack_in[u], 16)

            def load_slab(head, hh):
                v = bass.AP(tensor=d_line.tensor, offset=head * LINE, ap=[[1, P], [1, SLAB]])
                sp.dma_start(slab[:, hh, :], v).then_inc(slab_in[hh], 16)

            for u in range(UNITS):
                load_stack(u // 2, u)
                if u % 2 == 0:
                    load_slab(u // 2, u // 2)
            with sp.Fori(0, STEPS - 1) as it:
                for u in range(UNITS):
                    sp.wait_ge(qk_done, it * TILES + TPB * (u + 1))
                    load_stack(it * 2 + 2 + u // 2, u)
                    if u % 2 == 1:
                        sp.wait_ge(add_done, it * TILES + (ADD0 + TPB * (u + 1)))
                        load_slab(it * 2 + 2 + u // 2, u // 2)
            sp.wait_ge(qk_done, (STEPS - 1) * TILES + TPB)
            load_stack(0, 0)
            sp.wait_ge(add_done, ADD0 + STEPS * TILES)
            sp.wait_ge(qk_done, STEPS * TILES + AHEAD)
            sp.wait_ge(ffn_const, 1)
            for c in range(CC):
                sp.dma_start(w1[:, c, :].rearrange("p (e h) -> p e h", e=E),
                             ffn_w1[:, c * P:(c + 1) * P, :].rearrange("e p h -> p e h")).then_inc(ffn_in, 16)
            sp.dma_start(w2, ffn_w2.rearrange("(m a) h d -> (a h) m d", a=2)).then_inc(ffn_in, 16)
            for b in range(B):
                sp.dma_start(b2x[b * 64:b * 64 + 57:8, b, :], ffn_b2).then_inc(ffn_in, 16)
            for t in range(NT):
                sp.wait_ge(out_done, t + 1)
                sp.dma_start(out.rearrange("b (t p) c -> (b t) p c", p=P)[t], o_out[:, t % 4, 0:D]).then_inc(stored[t % 4], 16)
            for i in range(4):
                sp.wait_ge(stored[i], 16 * (NT // 4))

        @block.gpsimd
        def _(pool):
            step = Counter(pool, pool_step)
            for m in (ident, anti):
                step(pool.memset(m[:, :], 0.0))
            pool.memset(ones[:, :], 1.0).then_inc(const_step, 1)
            pool.memset(eps[:, :], LN_EPS).then_inc(const_step, 1)
            step(pool.affine_select(out=ident[:, :], in_=ident[:, :], compare_op=ALU.not_equal, fill=1.0,
                                    base=0, pattern=[[-1, P]], channel_multiplier=1))
            step(pool.affine_select(out=anti[:, :], in_=anti[:, :], compare_op=ALU.not_equal, fill=1.0,
                                    base=1 - P, pattern=[[1, P]], channel_multiplier=1))
            step(pool.memset(kbd, 0.0))
            step(pool.memset(vbd, 0.0))
            pool.sem_inc(const_ready, 1)
            step(pool.iota(ramp, pattern=[[1, RES]], base=0, channel_multiplier=-1, allow_small_or_imprecise_dtypes=True))
            step(pool.tensor_scalar(ramp, ramp, 0.0, None, ALU.max))
            step(pool.tensor_scalar(ramp, ramp, 1.0 / (RES - 1), None, ALU.mult))
            step(pool.memset(onehot, 1.0))
            for at, base, way in ((0, (RES - 1) * (S - 1), -1), (S, RES - 1, 1)):
                part = onehot[:, at:at + S]
                step(pool.affine_select(out=part, in_=part, compare_op=ALU.is_ge, fill=0.0, base=base + (S - 1) // 2,
                                        pattern=[[way * (RES - 1), S]], channel_multiplier=-(S - 1)))
                step(pool.affine_select(out=part, in_=part, compare_op=ALU.is_ge, fill=0.0, base=(S - 1) // 2 - base,
                                        pattern=[[-way * (RES - 1), S]], channel_multiplier=S - 1))
            step(pool.memset(norm_sel, 1.0))
            for e in range(2):
                part = norm_sel[:, e, :]
                step(pool.affine_select(out=part, in_=part, compare_op=ALU.is_ge, fill=0.0, base=P * e,
                                        pattern=[[-DH, 32]], channel_multiplier=1))
                step(pool.affine_select(out=part, in_=part, compare_op=ALU.is_ge, fill=0.0, base=DH - 1 - P * e,
                                        pattern=[[DH, 32]], channel_multiplier=-1))
            pool.sem_inc(const_ready, 1)
            for i, (half, n, e) in enumerate(proj_order):
                pool.wait_ge(resid_done, i + 1)
                p2 = parts[:, e, 1, n * 512:(n + 1) * 512]
                p3 = parts[:, e, 2, n * 512:(n + 1) * 512]
                step(pool.tensor_copy(p2, resid[:, i % 2, :]))
                pool.tensor_tensor(p3, resid[:, i % 2, :], p2, ALU.subtract).then_inc(part3_done, 1)
            after(pool, "xa", 7)
            after(pool, "vT", 1)
            step(pool.memset(v_all[:, :, :, DH:32], 0.0))
            pool.memset(v_all[:, :, :, DH:DH + 1], 1.0).then_inc(v_zeroed, 1)
            pool.wait_ge(v_zeroed, 1)
            after(pool, "norm", 7)
            pool.wait_ge(shift_done, 1)
            step(pool.memset(st_k[SHIFT_ROW:STACK, :, :], 1.0))

            def stage(head, u):
                b = u % 2
                return pool.tensor_copy(v_st[:, u, :, :], v_all[:, b * TPB:(b + 1) * TPB, :, :].rearrange(
                    "p t h d -> p t (h d)")[:, :, bass.ds(head * 32, 32)])

            taken(pool, index["v", NT // 2 - 1])
            for u in range(UNITS):
                stage(u // 2, u).then_inc(v_staged, 1)
            with pool.Fori(0, STEPS - 1) as it:
                for u in range(UNITS):
                    pool.wait_ge(pv_done, it * (TILES // 2) + (PV0 + 4 * (u + 1)))
                    pool.sem_inc(stage_go, 1)
                    stage(it * 2 + 2 + u // 2, u).then_inc(v_staged, 1)
            pool.wait_ge(add_done, ADD0 + STEPS * TILES)
            pool.wait_ge(qk_done, STEPS * TILES + AHEAD)
            pool.wait_ge(stack_in[0], 48 * (STEPS + 1))
            step(pool.memset(b2x, 0.0))
            step(pool.memset(pick, 1.0))
            for b in range(B):
                for m in range(NM):
                    for a in range(2):
                        part = pick[:, b * NM + m, a * SUB:(a + 1) * SUB]
                        row = b * 64 + (2 * m + a) * 8
                        step(pool.affine_select(out=part, in_=part, compare_op=ALU.is_equal, fill=0.0, base=-row,
                                                pattern=[[0, SUB]], channel_multiplier=1))
            step(pool.memset(block8, 1.0))
            blk = block8.rearrange("p (g c) -> p g c", c=8)
            step(pool.affine_select(out=blk, in_=blk, compare_op=ALU.is_ge, fill=0.0, base=0,
                                    pattern=[[-8, 16], [0, 8]], channel_multiplier=1))
            step(pool.affine_select(out=blk, in_=blk, compare_op=ALU.is_ge, fill=0.0, base=7,
                                    pattern=[[8, 16], [0, 8]], channel_multiplier=-1))
            step(pool.iota(expw, pattern=[[-1, E]], base=E, channel_multiplier=0, allow_small_or_imprecise_dtypes=True))
            step(pool.iota(r_s[:, 12:13].bitcast(I32), pattern=[[0, 1]], base=0, channel_multiplier=1))
            pool.sem_inc(ffn_const, 1)
            for g in range(4):
                pool.wait_ge(ln_done, 4 + g + 1)
                pool.tensor_tensor(xt[:, 4 * g:4 * g + 4, :], xt[:, 4 * g:4 * g + 4, :],
                                   bo_bc[:, :].unsqueeze(1).broadcast_to([P, 4, D]), ALU.add).then_inc(bo_added, 1)
            for t in range(NT):
                pool.wait_ge(xrecip_done, t + 1)
                if t >= 2:
                    after(pool, "xpT", (t - 2, 1))
                pool.tensor_tensor(xp[:, t % 2, :].rearrange("p (h k) -> p h k", h=XH),
                                   xe[:, t % 2, :].rearrange("p (h k) -> p h k", h=XH),
                                   x_s[:, 1, t % 4, :].unsqueeze(2).broadcast_to([P, XH, KV]),
                                   ALU.mult).then_inc(xprob_done, 1)

        @block.scalar
        def _(act):
            act.dma_start(coef_sb, coeffs).then_inc(small_in, 16)
            with nc.allow_non_contiguous_dma("64 elements"):
                act.dma_start(wposT, w_pos.rearrange("h f -> f h")).then_inc(small_in, 16)
                act.dma_start(b1_sb[:, :], ffn_b1.rearrange("(m a) h -> (a h) m", a=2)).then_inc(small_in, 16)
                act.dma_start(gb_sb[:, :], gate_b.rearrange("(e a) -> e a", a=1)).then_inc(small_in, 16)
            act.dma_start(gw_sb[:, :, :], gate_w.rearrange("(c p) e -> p c e", p=P)).then_inc(gate_in, 16)
            act.dma_start(ctx_nat, ctx_in.rearrange("b k c -> (b k) c")).then_inc(small_in, 16)
            act.dma_start(bo_bc[:, :], xb_o.rearrange("(a c) -> a c", a=1).broadcast_to([P, D])).then_inc(small_in, 16)

            def copy(name, key, dst, **kw):
                act.activation(dst, result(act, name, key), ACT.Copy, **kw).then_inc(act_took, 1)

            def root(n):
                act.wait_ge(ln_var, n + 1)
                act.activation(ln_s[:, 1, :], ln_s[:, 0, :], ACT.Sqrt).then_inc(ln_sd, 1)

            for g in range(2):
                root(g)
            wT_f = wT[:, :, :].rearrange("p a b -> p (a b)")
            for n in range(3):
                copy("wT", n, wT_f[:, n * 512:(n + 1) * 512])
            copy("woT", 0, woT[:, :, :].rearrange("p a b -> p (a b)"))
            wqT_f = wqT.rearrange("p a b -> p (a b)")
            for n in range(4):
                copy("wqT", n, wqT_f[:, n * 512:(n + 1) * 512])
            b_ = result(act, "ctxT", 0)
            act.activation(ctxT[:, 0, :], b_[:, 0:P], ACT.Copy).then_inc(act_step, 1)
            act.activation(ctxT[0:DC - P, 1, :], b_[0:DC - P, P:2 * P], ACT.Copy).then_inc(act_took, 1)
            act.wait_ge(const_ready, 1)
            for n in range(2):
                b_ = result(act, "kT", n)
                for hl in range(2):
                    rows = slice(64 * hl, 64 * hl + 64)
                    for b in range(B):
                        ins = act.activation(kbd[rows, b * NK + 4 * n:b * NK + 4 * n + 4, 64 * hl:64 * hl + 64],
                                             b_[rows, :].rearrange("p (k c) -> p k c", k=4)[:, :, b * KV:(b + 1) * KV],
                                             ACT.Copy)
                        ins.then_inc(act_took if hl and b else act_step, 1)
            xa_f = xa[:, :, :, :].rearrange("p c b n -> p (c b n)")
            for n in range(8):
                copy("xa", n, xa_f[:, n * 512:(n + 1) * 512])
            for g in range(4):
                if g >= 2:
                    root(g)
                for c in range(CC):
                    copy("lnT", (g, c), lnT[:, c, g * 512:(g + 1) * 512])
            for i, (half, n, e) in enumerate(proj_order):
                b_ = result(act, "proj", (half, n, e))
                scale = SCALE if half == 0 else 1.0
                if i >= 4:
                    after(act, "norm", i // 2 - 2)
                act.activation(sq[:, i % 4, :], b_, ACT.Square, scale=scale).then_inc(part1_done, 1)
                if half == 1 and n == 0 and e == 0:
                    act.wait_ge(region_ready, 1)
                act.activation(parts[:, e, 0, n * 512:(n + 1) * 512], b_, ACT.Copy, scale=scale).then_inc(part1_done, 1)
            act.wait_ge(bound_done, 1)
            for b in range(B):
                act.activation(shift[:, b * S:(b + 1) * S], qn2[:, b * S:(b + 1) * S], ACT.Sqrt,
                               scale=head_s[:, 4 + b:5 + b]).then_inc(root_done, 1)
            act.wait_ge(v_zeroed, 1)
            for n in range(NT // 2):
                act.activation(v_all[:, 2 * n:2 * n + 2, :, 0:DH],
                               result(act, "v", n).rearrange("p (t h d) -> p t h d", t=2, h=H),
                               ACT.Copy).then_inc(act_took, 1)

            def heads(o):
                return act.activation(o_sb[:, o, :], ps[:, 6 + o, 0:D], ACT.Copy).then_inc(heads_out, 1)

            act.sem_inc(heads_out, OUT0)
            with act.Fori(0, STEPS) as it:
                for u in range(UNITS):
                    for q in range(4):
                        c = 4 * u + q
                        act.wait_ge(add_done, it * TILES + (ADD0 + 2 * (c + 1)))
                        act.activation(ring[:, c % RING, :], ring[:, c % RING, :], ACT.Exp).then_inc(exp_done, 1)
                        if q == 1:
                            act.wait_ge(pv_done, it * (TILES // 2) + (PV0 + 4 * u))
                            heads((u - 1) % 2)
            act.wait_ge(pv_done, STEPS * (TILES // 2) + PV0)
            heads((UNITS - 1) % 2)

            for g in range(4):
                for c in range(CC):
                    copy("oT", (g, c), lnT[:, c, g * 512:(g + 1) * 512])
            for g in range(4):
                root(4 + g)
                for c in range(CC):
                    copy("ln2T", (g, c), lnT[:, c, g * 512:(g + 1) * 512])
            for t in range(NT + XLAG):
                if t < NT:
                    act.wait_ge(centred, 2 * t + 2)
                    if t >= 2:
                        act.wait_ge(xprob_done, t - 1)
                    act.activation(xe[:, t % 2, :], xd[:, t % 2, :], ACT.Exp, scale=XSCALE).then_inc(xexp_done, 1)
                if t >= XLAG:
                    k = t - XLAG
                    for hf in range(2):
                        if k >= 2 and hf == 0:
                            after(act, "xo", k - 2)
                        copy("xpT", (k, hf), xpT[:, k % 2, hf * 512:(hf + 1) * 512])
            for g in range(4):
                root(8 + g)
                for c in range(CC):
                    copy("ln3T", (g, c), lnT[:, c, g * 512:(g + 1) * 512])
            for n in range(4):
                act.activation(gT[:, n * 512:(n + 1) * 512], result(act, "gate", n)[0:E, :], ACT.Identity,
                               bias=gb_sb[:, 0:1]).then_inc(act_took, 1)
            act.wait_ge(centred, 2 * NT + 1)
            act.activation(gates[:, 1, :], gates[:, 0, :], ACT.Exp).then_inc(xexp_done, 1)
            for m, n in w1_order:
                act.activation(hid[:, m, n * 512:(n + 1) * 512], result(act, "w1", (m, n)), ACT.Gelu,
                               bias=b1_sb[:, m:m + 1]).then_inc(act_took, 1)

        @block.tensor
        def _(pe):
            def end(ins):
                ins.then_inc(job_done, 1)

            def turn4(name, key, ins_):
                b_ = job(pe, name, key)
                for src, m, at in ins_:
                    last = pe.transpose(b_[0:src.shape[1], at:at + P], src, m[:, :])
                end(last)

            pe.wait_ge(const_ready, 1)
            pe.wait_ge(w_in, 32)
            for n in range(3):
                turn4("wT", n, [(w_nat[:, (4 * n + i) % 6, ((4 * n + i) // 6) * P:((4 * n + i) // 6 + 1) * P], ident, i * P)
                                for i in range(4)])
            turn4("woT", 0, [(wo_nat[:, i % 2, (i // 2) * P:(i // 2 + 1) * P], ident, i * P) for i in range(4)])
            pe.wait_ge(xw_in, 80)
            for n in range(4):
                turn4("wqT", n, [(wq_nat[:, i % 2, (2 * n + i // 2) * P:(2 * n + i // 2 + 1) * P], ident, i * P)
                                 for i in range(4)])
            pe.wait_ge(small_in, 96)
            turn4("ctxT", 0, [(ctx_nat[:, 0:P], ident, 0), (ctx_nat[:, P:DC], ident, P)])
            taken(pe, index["ctxT", 0])
            for name, w in (("kT", wk_nat), ("vT", wv_nat)):
                for n in range(2):
                    b_ = job(pe, name, n)
                    for i in range(4):
                        k = 4 * n + i
                        pe.matmul(b_[:, i * P:(i + 1) * P], w[:, 0, k * P:(k + 1) * P], ctxT[:, 0, :],
                                  start=True, stop=False, skip_group_check=True)
                        last = pe.matmul(b_[:, i * P:(i + 1) * P], w[0:DC - P, 1, k * P:(k + 1) * P], ctxT[0:DC - P, 1, :],
                                         start=False, stop=True, skip_group_check=True)
                    end(last)
            taken(pe, index["kT", 1])
            for n in range(8):
                c, b, k0 = n // 4, n // 2 % 2, 4 * (n % 2)
                b_ = job(pe, "xa", n)
                for i in range(4):
                    last = pe.matmul(b_[:, i * P:(i + 1) * P], wqT[:, k0 + i, c * P:(c + 1) * P], kbd[:, b * NK + k0 + i, :],
                                     start=True, stop=True, skip_group_check=True)
                end(last)
            taken(pe, index["vT", 1])
            pe.wait_ge(xwo_in, 16)
            for n in range(8):
                b_ = job(pe, "xvw", n)
                for i in range(2):
                    last = pe.matmul(b_[:, i * D:(i + 1) * D], vbd[:, 2 * n + i, :], xwo[:, (2 * n + i) % NK, :],
                                     start=True, stop=True, skip_group_check=True)
                end(last)
            pe.wait_ge(const_ready, 2)
            end(pe.matmul(job(pe, "ceff", 0)[0:TAPS, 0:H], coef_sb, wposT, start=True, stop=True))
            taken(pe, index["ceff", 0])
            end(pe.matmul(job(pe, "biasT", 0)[:, 0:H], ramp, ceff, start=True, stop=True))
            taken(pe, index["biasT", 0])
            for n in range(4):
                end(pe.matmul(job(pe, "line", n)[0:H, :], biasT, onehot[:, n * 512:(n + 1) * 512], start=True, stop=True))
            for g in range(4):
                pe.wait_ge(ln_done, g + 1)
                for c in range(CC):
                    turn4("lnT", (g, c), [(xn[:, g % 2, i, c * P:(c + 1) * P], ident, i * P) for i in range(4)])
                for c in range(CC):
                    turn4("lnTr", (g, c), [(xn[:, g % 2, i, c * P:(c + 1) * P], anti, (3 - i) * P) for i in range(4)])
            taken(pe, index["lnT", (3, 1)])
            taken(pe, index["lnTr", (3, 1)])

            def norm(k):
                pe.wait_ge(part1_done, 4 * k + 3)
                b_ = job(pe, "norm", k)
                for e in range(2):
                    last = pe.matmul(b_[0:32, :], norm_sel[:, e, :], sq[:, (2 * k + e) % 4, :],
                                     start=(e == 0), stop=(e == 1))
                end(last)

            for i, (half, n, e) in enumerate(proj_order):
                b_ = job(pe, "proj", (half, n, e))
                src = lnTr if half else lnT
                for c in range(CC):
                    last = pe.matmul(b_, wT[:, c, half * D + e * P:half * D + (e + 1) * P],
                                     src[:, c, n * 512:(n + 1) * 512], start=(c == 0), stop=(c == CC - 1))
                end(last)
                if e == 1 and i > 1:
                    norm(i // 2 - 1)
            norm(7)
            for n in range(NT // 2):
                b_ = job(pe, "v", n)
                for i in range(2):
                    for c in range(CC):
                        last = pe.matmul(b_[:, i * D:(i + 1) * D], lnTr[:, c, (2 * n + i) * P:(2 * n + i + 1) * P],
                                         wT[:, c, 2 * D:3 * D], start=(c == 0), stop=(c == CC - 1), skip_group_check=True)
                end(last)

            def scores(it, g):
                gi = g % TILES
                u, jt = gi // TPB, gi % TPB
                if jt == 0:
                    pe.wait_ge(stack_in[u], it * 48 + 48 * (1 + g // TILES))
                pe.wait_ge(add_done, it * TILES + (ADD0 + g - before[gi] + 1))
                for q in range(2):
                    last = pe.matmul(ps[:, 2 * slot_of[gi] + q, :], st_k[0:STACK, u, jt * P:(jt + 1) * P],
                                     st_q[0:STACK, u, q * 512:(q + 1) * 512], start=True, stop=True)
                last.then_inc(qk_done, 1)

            def weighted(it, g):
                u, jt = g // TPB, g % TPB
                o = u % 2
                if jt == 0:
                    pe.wait_ge(v_staged, it * UNITS + u + 1)
                    pe.wait_ge(finished, it * UNITS + (u + FIN0))
                if g % 2 == 0:
                    pe.wait_ge(exp_done, it * (TILES // 2) + g // 2 + 1)
                for c in range(4):
                    last = pe.matmul(ps[32 * c:32 * c + 32, 6 + o, 0:D], v_st[:, u, jt, :],
                                     ring[:, g // 2 % RING, (g % 2) * S + c * D:(g % 2) * S + (c + 1) * D],
                                     start=(jt == 0), stop=(jt == TPB - 1), skip_group_check=True)
                if g % 2:
                    last.then_inc(pv_done, 1)

            def turn(wait, o):
                pe.wait_ge(heads_out, wait)
                for t in range(2):
                    last = pe.transpose(ps[:, 6 + o, D + t * P:D + (t + 1) * P], o_sb[:, o, t * P:(t + 1) * P], ident[:, :])
                last.then_inc(turned, 1)

            taken(pe, index["v", NT // 2 - 1])
            for t in range(2):
                last = pe.matmul(ps[:, 7, t * P:(t + 1) * P], ones[:, :], ones[:, :], start=True, stop=True,
                                 skip_group_check=True)
            last.then_inc(pv_done, PV0)
            for g in range(AHEAD):
                scores(0, g)
            with pe.Fori(0, STEPS) as it:
                for g in range(TILES):
                    scores(it, g + AHEAD)
                    weighted(it, g)
                    if g % TPB == 3:
                        turn(it * UNITS + (g // TPB + OUT0 + 1), (g // TPB + 1) % 2)
            turn(STEPS * UNITS + OUT0 + 1, 1)
            pe.wait_ge(add_done, ADD0 + STEPS * TILES)
            pe.wait_ge(finished, STEPS * UNITS + FIN0 + 1)

            for g in range(4):
                for c in range(CC):
                    turn4("oT", (g, c), [(o_all[:, 4 * g + i, DH + c * P:DH + (c + 1) * P], ident, i * P) for i in range(4)])
            for n in range(NT // 2):
                if n % 2 == 0:
                    taken(pe, index["oT", (n // 2, 1)])
                b_ = job(pe, "wo", n)
                for i in range(2):
                    for c in range(CC):
                        last = pe.matmul(b_[:, i * D:(i + 1) * D], lnT[:, c, (2 * n + i) * P:(2 * n + i + 1) * P],
                                         woT[:, c, :], start=(c == 0), stop=(c == CC - 1), skip_group_check=True)
                end(last)
            for g in range(4):
                pe.wait_ge(ln_done, 4 + g + 1)
                for c in range(CC):
                    turn4("ln2T", (g, c), [(xn[:, g % 2, i, c * P:(c + 1) * P], ident, i * P) for i in range(4)])
            for t in range(NT + XLAG):
                if t < NT:
                    if t % 4 == 0:
                        taken(pe, index["ln2T", (t // 4, 1)])
                    for hf in range(2):
                        b_ = job(pe, "xl", (t, hf))
                        for c in range(CC):
                            last = pe.matmul(b_, lnT[:, c, t * P:(t + 1) * P],
                                             xa[:, c, t // TPB, hf * 512:(hf + 1) * 512], start=(c == 0), stop=(c == CC - 1))
                        end(last)
                if t >= XLAG:
                    k = t - XLAG
                    pe.wait_ge(xprob_done, k + 1)
                    for hf in range(2):
                        turn4("xpT", (k, hf), [(xp[:, k % 2, hf * 512 + i * P:hf * 512 + (i + 1) * P], ident, i * P)
                                               for i in range(4)])
                    b_ = job(pe, "xo", k)
                    taken(pe, index["xpT", (k, 1)])
                    for i in range(NK):
                        last = pe.matmul(b_[:, 0:D], xpT[:, k % 2, i * P:(i + 1) * P], xvw[:, k // TPB, i, :],
                                         start=(i == 0), stop=(i == NK - 1))
                    end(last)
            for g in range(4):
                pe.wait_ge(ln_done, 8 + g + 1)
                for c in range(CC):
                    turn4("ln3T", (g, c), [(xn[:, g % 2, i, c * P:(c + 1) * P], ident, i * P) for i in range(4)])
            taken(pe, index["ln3T", (3, 1)])
            pe.wait_ge(gate_in, 16)
            for n in range(4):
                b_ = job(pe, "gate", n)
                for c in range(CC):
                    last = pe.matmul(b_[0:E, :], gw_sb[:, c, :], lnT[:, c, n * 512:(n + 1) * 512],
                                     start=(c == 0), stop=(c == CC - 1))
                end(last)
            b_ = job(pe, "gateT", 0)
            taken(pe, index["gate", 3])
            for t in range(NT):
                last = pe.transpose(b_[:, t * E:(t + 1) * E], gT[:, t * P:(t + 1) * P], ident[0:E, 0:E])
            end(last)

            def hidden(key):
                m, n = key
                b_ = job(pe, "w1", key)
                for c in range(CC):
                    last = pe.matmul(b_, w1[:, c, m * P:(m + 1) * P], lnT[:, c, n * 512:(n + 1) * 512],
                                     start=(c == 0), stop=(c == CC - 1))
                end(last)

            pe.wait_ge(ffn_in, 80)
            for k in w1_order[:5]:
                hidden(k)
            pe.wait_ge(rrep_done, 1)
            for n in range(2):
                turn4("rrep", n, [(rrep[:, 4 * n + i, :], ident, i * P) for i in range(4)])
            for i in range(10):
                b_ = job(pe, "digit", i)
                pe.wait_ge(digit_asked, i + 1)
                end(pe.matmul(b_[:, 0:1], block8, r_s[:, 8:9].bitcast(BF16)[:, 0:1], start=True, stop=True))
                hidden(w1_order[5 + i])
            for k in w1_order[15:]:
                hidden(k)
            pe.wait_ge(chosen, 1)
            for m, n in w1_order:
                end(pe.matmul(job(pe, "mask", (m, n)), pick[:, (n // 2) * NM + m, :],
                              sel_b[:, (n % 2) * 512:(n % 2 + 1) * 512], start=True, stop=True))
            taken(pe, index["mask", (NM - 1, 3)])
            for t in range(NT):
                b_ = job(pe, "w2", t)
                for m in range(NM):
                    pe.matmul(b_[:, 0:D], hid[:, m, t * P:(t + 1) * P], w2[:, m, :], start=(m == 0), stop=False)
                end(pe.matmul(b_[:, 0:D], sel_f[:, (t % TPB) * P:(t % TPB + 1) * P], b2x[:, t // TPB, :],
                              start=False, stop=True))

        @block.vector
        def _(dve):
            step = Counter(dve, dve_step)

            def layer_norm(n):
                g = n % 4
                for i in range(4):
                    dve.bn_stats(st[:, i, :], xt[:, 4 * g + i, :]).then_inc(dve_step, 1)
                    step.n += 1
                dve.wait_ge(dve_step, step.n)
                for i in range(4):
                    ins = dve.bn_aggr(mv[:, i, :], st[:, i, :])
                    ins.then_inc(dve_step, 1)
                    step.n += 1
                dve.wait_ge(dve_step, step.n)
                var, sd, r, a, b_ = (ln_s[:, i, :] for i in range(5))
                dve.tensor_scalar(var, mv[:, :, 1], LN_EPS, None, ALU.add).then_inc(ln_var, 1)
                dve.wait_ge(ln_sd, n + 1)
                step(dve.reciprocal(r, sd))
                step(dve.tensor_tensor(a, r, r, ALU.mult))
                step(dve.tensor_tensor(b_, a, var, ALU.mult))
                step(dve.tensor_scalar(a, b_, -0.5, 1.5, ALU.mult, ALU.add))
                step(dve.tensor_tensor(b_, r, a, ALU.mult))
                if n % 4 >= 2:
                    after(dve, *{0: ("lnTr", (g - 2, 1)), 1: ("ln2T", (g - 2, 1)), 2: ("ln3T", (g - 2, 1))}[n // 4])
                elif n >= 4:
                    after(dve, *{1: ("lnTr", (g + 2, 1)), 2: ("ln2T", (g + 2, 1))}[n // 4])
                for i in range(4):
                    ins = dve.tensor_scalar(xn[:, g % 2, i, :], xt[:, 4 * g + i, :], mv[:, i, 0:1], b_[:, i:i + 1],
                                            ALU.subtract, ALU.mult)
                    if i == 3:
                        ins.then_inc(ln_done, 1)
                dve.wait_ge(ln_done, n + 1)

            for g in range(2):
                dve.wait_ge(x_in[g], 16)
                layer_norm(g)
            dve.wait_ge(const_ready, 1)
            for n in range(2):
                b_ = result(dve, "vT", n)
                for hl in range(2):
                    rows = slice(64 * hl, 64 * hl + 64)
                    ins = dve.tensor_copy(
                        vbd.rearrange("p (b k) c -> p b k c", b=B)[rows, :, 4 * n:4 * n + 4, 64 * hl:64 * hl + 64],
                        b_[rows, :].rearrange("p (k b c) -> p b k c", k=4, b=B))
                ins.then_inc(dve_took, 1)
            xvw_2 = xvw_f.rearrange("p (n c) -> p n c", n=8)
            for n in range(8):
                dve.tensor_copy(xvw_2[:, n, :], result(dve, "xvw", n)).then_inc(dve_took, 1)
            dve.tensor_copy(ceff, result(dve, "ceff", 0)[0:TAPS, 0:H]).then_inc(dve_took, 1)
            dve.tensor_copy(biasT, result(dve, "biasT", 0)[:, 0:H]).then_inc(dve_took, 1)
            for n in range(4):
                dve.tensor_copy(line_sb[:, n * 512:(n + 1) * 512], result(dve, "line", n)[0:H, :]).then_inc(dve_took, 1)
            taken(dve, index["line", 3])
            step(dve.tensor_reduce(head_s[:, 6:7], line_sb, AX.X, ALU.max))
            dve.sem_inc(line_done, 1)
            for g in range(4):
                if g >= 2:
                    dve.wait_ge(x_in[g], 16)
                    layer_norm(g)
                if g >= 1:
                    for c in range(CC):
                        dve.tensor_copy(lnTr[:, c, lnr_at[g - 1]:lnr_at[g - 1] + 512],
                                        result(dve, "lnTr", (g - 1, c))).then_inc(dve_took, 1)
            for c in range(CC):
                dve.tensor_copy(lnTr[:, c, lnr_at[3]:lnr_at[3] + 512], result(dve, "lnTr", (3, c))).then_inc(dve_took, 1)

            def take_norm(k):
                b_ = result(dve, "norm", k)[0:H, :]
                if k < 4:
                    dve.tensor_copy(qn2[:, k * 512:(k + 1) * 512], b_).then_inc(dve_took, 1)
                else:
                    dve.tensor_reduce(head_s[:, k - 4:k - 3], b_, AX.X, ALU.max).then_inc(dve_took, 1)

            for i, (half, n, e) in enumerate(proj_order):
                dve.wait_ge(part1_done, 2 * i + 2)
                if i >= 2:
                    dve.wait_ge(part3_done, i - 1)
                j = index["proj", (half, n, e)]
                dve.scalar_tensor_tensor(out=resid[:, i % 2, :], in0=bank(j), scalar=SCALE if half == 0 else 1.0,
                                         in1=parts[:, e, 0, n * 512:(n + 1) * 512], op0=ALU.mult,
                                         op1=ALU.subtract).then_inc(resid_done, 1)
                dve.wait_ge(resid_done, i + 1)
                dve.sem_inc(dve_took, 1)
                if e == 1 and i > 1:
                    take_norm(i // 2 - 1)
            take_norm(7)
            taken(dve, index["norm", 7])
            step(dve.tensor_reduce(head_s[:, 4:6], head_s[:, 0:4].rearrange("p (b n) -> p b n", b=B), AX.X, ALU.max))
            dve.tensor_scalar(head_s[:, 4:6], head_s[:, 4:6], UMARGIN, None, ALU.mult).then_inc(bound_done, 1)
            dve.wait_ge(root_done, 2)
            step(dve.tensor_scalar(shift, shift, head_s[:, 6:7], -1.0, ALU.add, ALU.mult))
            step(dve.tensor_copy(shift_p[:, 0, :], shift))
            step(dve.tensor_tensor(shift, shift, shift_p[:, 0, :], ALU.subtract))
            dve.tensor_copy(shift_p[:, 1, :], shift).then_inc(shift_done, 1)

            def finish(col, n, b, o):
                heads = ps[:, 6 + o, D:2 * D].rearrange("p (t c d) -> p t c d", t=2, c=4)
                dve.wait_ge(turned, n)
                dve.reciprocal(rs[:, :, :], heads[:, :, :, DH]).then_inc(attn_step, 1)
                dve.wait_ge(attn_step, n * 2 - 1)
                dve.tensor_tensor(low[:, :, :], low[:, :, :], rs[:, :, :], ALU.max).then_inc(attn_step, 1)
                dst = o_all[:, b * TPB:(b + 1) * TPB, :].rearrange("p (c t) k -> p t c k", t=2)[:, :, :, bass.ds(col, DH)]
                dve.tensor_tensor(dst, heads[:, :, :, 0:DH], rs[:, :, :].unsqueeze(3).broadcast_to([P, 2, 4, DH]),
                                  ALU.mult).then_inc(finished, 1)
                dve.wait_ge(attn_step, n * 2)

            step(dve.memset(low[:, :, :], 0.0))
            dve.sem_inc(add_done, ADD0)
            dve.sem_inc(finished, FIN0)
            with dve.Fori(0, STEPS) as it:
                for g in range(TILES):
                    u, jt = g // TPB, g % TPB
                    if g % (2 * TPB) == 0:
                        dve.wait_ge(slab_in[u // 2], it * 16 + 16)
                    dve.wait_ge(qk_done, it * TILES + g + 1)
                    if g % 2 == 0:
                        dve.wait_ge(pv_done, it * (TILES // 2) + (g // 2 - RING + PV0 + 1))
                    s0 = 2 * slot_of[g]
                    dve.tensor_tensor(ring[:, g // 2 % RING, (g % 2) * S:(g % 2 + 1) * S],
                                      ps[:, s0:s0 + 2, :].rearrange("p a b -> p (a b)"),
                                      slab[:, u // 2, jt * P:jt * P + S], ALU.add).then_inc(add_done, 1)
                    if jt == TPB - 1:
                        finish((it * 2 + (u + 1) // 2) * DH, it * UNITS + u + 1, (u - 1) % 2, (u - 1) % 2)
            dve.wait_ge(add_done, ADD0 + STEPS * TILES)
            dve.sem_inc(add_done, AHEAD - 3)
            dve.wait_ge(finished, STEPS * UNITS + FIN0)
            finish(H * DH, STEPS * UNITS + 1, 1, 1)

            for n in range(NT // 2):
                dve.tensor_tensor(xt[:, 2 * n:2 * n + 2, :].rearrange("p a b -> p (a b)"), result(dve, "wo", n),
                                  xt[:, 2 * n:2 * n + 2, :].rearrange("p a b -> p (a b)"), ALU.add).then_inc(dve_took, 1)
                if n % 2:
                    taken(dve, index["wo", n])
                    layer_norm(4 + n // 2)

            def centre(t):
                for hf in range(2):
                    b_ = result(dve, "xl", (t, hf)).rearrange("p (h k) -> p h k", k=KV)
                    m = x_s[:, 0, t % 4, 8 * hf:8 * hf + 8]
                    step(dve.tensor_reduce(m, b_, AX.X, ALU.max))
                    if t >= 2:
                        dve.wait_ge(xexp_done, t - 1)
                    dve.tensor_tensor(xd[:, t % 2, hf * 512:(hf + 1) * 512].rearrange("p (h k) -> p h k", k=KV), b_,
                                      m.unsqueeze(2).broadcast_to([P, 8, KV]), ALU.subtract).then_inc(centred, 1)
                    dve.wait_ge(centred, 2 * t + hf + 1)
                    dve.sem_inc(dve_took, 1)

            def sums(t):
                dve.wait_ge(xexp_done, t + 1)
                step(dve.tensor_reduce(x_s[:, 1, t % 4, :], xe[:, t % 2, :].rearrange("p (h k) -> p h k", k=KV), AX.X, ALU.add))
                dve.reciprocal(x_s[:, 1, t % 4, :], x_s[:, 1, t % 4, :]).then_inc(xrecip_done, 1)

            for t in range(NT + XLAG):
                if t < NT:
                    centre(t)
                    if t >= 1:
                        sums(t - 1)
                if t == NT:
                    sums(NT - 1)
                if t >= XLAG:
                    k = t - XLAG
                    if k % 4 == 0:
                        dve.wait_ge(bo_added, k // 4 + 1)
                    b_ = result(dve, "xo", k)
                    dve.tensor_tensor(xt[:, k, :], b_[:, 0:D], xt[:, k, :], ALU.add).then_inc(dve_took, 1)
            taken(dve, index["xo", NT - 1])
            for g in range(4):
                layer_norm(8 + g)

            dve.wait_ge(ffn_const, 1)
            g_ = [gates[:, i, :].rearrange("p (t e) -> p t e", e=E) for i in range(4)]
            small = r_s[:, 0:1]
            m16 = ln_s[:, 0:4, :].rearrange("p a b -> p (a b)")
            wb = expw.unsqueeze(1).broadcast_to([P, NT, E])

            def wide(v):
                return v.unsqueeze(2).broadcast_to([P, NT, E])

            step(dve.tensor_copy(g_[2], result(dve, "gateT", 0)[:, 0:NT * E].rearrange("p (t e) -> p t e", e=E)))
            dve.sem_inc(dve_took, 1)
            step(dve.tensor_reduce(m16, g_[2], AX.X, ALU.max))
            dve.tensor_tensor(g_[0], g_[2], wide(m16), ALU.subtract).then_inc(centred, 1)
            dve.wait_ge(xexp_done, NT + 1)
            step(dve.tensor_reduce(m16, g_[1], AX.X, ALU.add))
            step(dve.reciprocal(m16, m16))
            step(dve.tensor_tensor(g_[1], g_[1], wide(m16), ALU.mult))
            step(dve.memset(gates[:, 3, :], 0.0))
            step(dve.tensor_copy(g_[0], g_[1]))
            for k in range(TOPK):
                step(dve.tensor_reduce(m16, g_[0], AX.X, ALU.max))
                step(dve.tensor_tensor(g_[2], g_[0], wide(m16), ALU.is_equal))
                step(dve.tensor_tensor(g_[2], g_[2], wb, ALU.mult))
                step(dve.tensor_reduce(m16, g_[2], AX.X, ALU.max))
                step(dve.tensor_tensor(g_[2], wide(m16), wb, ALU.is_equal))
                step(dve.tensor_tensor(g_[3], g_[3], g_[2], ALU.add))
                step(dve.scalar_tensor_tensor(out=gates[:, 0, :], in0=gates[:, 2, :], scalar=-2.0, in1=gates[:, 0, :],
                                              op0=ALU.mult, op1=ALU.add))
            step(dve.tensor_tensor(g_[1], g_[1], g_[3], ALU.mult))
            half = NT * E // B
            step(dve.tensor_tensor(gates[:, 0, 0:half], gates[:, 1, 0:half], gates[:, 1, half:2 * half], ALU.add))
            step(dve.tensor_scalar(gates[:, 0, 0:half], gates[:, 0, 0:half], DEN_EPS, None, ALU.add))
            step(dve.reciprocal(gates[:, 0, 0:half], gates[:, 0, 0:half]))
            for b in range(B):
                step(dve.tensor_tensor(gates[:, 2, b * half:(b + 1) * half], gates[:, 1, b * half:(b + 1) * half],
                                       gates[:, 0, 0:half], ALU.mult))
            for b in range(B):
                v = g_[2][:, b * TPB:(b + 1) * TPB, :].unsqueeze(3).broadcast_to([P, TPB, E, 8])
                step(dve.tensor_copy(rrep[:, :, b * 64:(b + 1) * 64].rearrange("p t (e c) -> p t e c", c=8), v))
            dve.sem_inc(rrep_done, 1)
            lane = r_s[:, 12:13].bitcast(I32)
            step(dve.tensor_scalar(lane, lane, 7, None, ALU.bitwise_and))
            for i in range(10):
                step(dve.tensor_scalar(digits[:, i:i + 1].bitcast(I32), lane, 27 - 3 * i, None, ALU.logical_shift_left))
            for n in range(2):
                dve.tensor_copy(rr[:, n * 512:(n + 1) * 512], result(dve, "rrep", n)).then_inc(dve_took, 1)
            thr, cand, count, ask, got = (r_s[:, i:i + 1] for i in (1, 2, 3, 8, 5))
            step(dve.memset(thr, 0.0))
            taken(dve, index["rrep", 1])
            for i in range(10):
                step(dve.tensor_tensor(cand.bitcast(U32), thr.bitcast(U32), digits[:, i:i + 1], ALU.bitwise_or))
                step(dve.tensor_scalar(junk, rr, cand, None, ALU.is_ge, ALU.add, accum_out=count))
                dve.tensor_scalar(ask.bitcast(BF16)[:, 0:1], count, float(KSEL), None, ALU.is_ge).then_inc(digit_asked, 1)
                b_ = result(dve, "digit", i)
                step(dve.tensor_scalar(got.bitcast(U32), b_[:, 0:1], -1.0, float(1 << (27 - 3 * i)), ALU.add, ALU.mult))
                dve.sem_inc(dve_took, 1)
                step(dve.tensor_tensor(thr.bitcast(U32), thr.bitcast(U32), got.bitcast(U32), ALU.bitwise_or))
            step(dve.tensor_scalar(above, rr, thr, None, ALU.is_gt, ALU.add, accum_out=count))
            step(dve.tensor_scalar(count, count, -1.0, float(KSEL), ALU.mult, ALU.add))
            step(dve.tensor_scalar(rr, rr, thr, None, ALU.is_equal))
            step(dve.tensor_tensor_scan(prefix, rr, rr, 0.0, ALU.add, ALU.bypass))
            step(dve.scalar_tensor_tensor(out=prefix, in0=prefix, scalar=count, in1=rr, op0=ALU.is_le, op1=ALU.mult))
            step(dve.tensor_tensor(sel_f, above, prefix, ALU.add))
            dve.tensor_copy(sel_b, sel_f).then_inc(chosen, 1)

            for m, n in w1_order:
                taken(dve, index["w1", (m, n)])
                h_ = hid[:, m, n * 512:(n + 1) * 512]
                dve.tensor_tensor(h_, result(dve, "mask", (m, n)), h_, ALU.mult).then_inc(dve_took, 1)
            for t in range(NT):
                if t == 0:
                    after(dve, "ln3T", (3, 1))
                if t >= 4:
                    dve.wait_ge(stored[t % 4], 16 * (t // 4))
                dve.tensor_tensor(o_out[:, t % 4, 0:D], result(dve, "w2", t)[:, 0:D], xt[:, t, :], ALU.add).then_inc(out_done, 1)
                dve.wait_ge(out_done, t + 1)
                dve.sem_inc(dve_took, 1)


_INS = ["x", "ctx_768", "L0_attn_Wqkv", "L0_attn_Wout", "L0_attn_Wpos", "L0_attn_coeffs", "L0_xattn_w_q",
        "L0_xattn_w_k", "L0_xattn_w_v", "L0_xattn_w_out", "L0_xattn_b_out", "L0_ffn_w_gate_w", "L0_ffn_w_gate_b",
        "L0_ffn_W1", "L0_ffn_b1", "L0_ffn_W2", "L0_ffn_b2"]
_OUTS = [((B, S, D), "float32")]


def kernel(**inputs):
    import numpy as _np
    import concourse.bacc as _bacc
    from concourse import mybir as _mybir
    from concourse.bass_utils import run_bass_kernel_spmd as _run

    nc = _bacc.Bacc("TRN2", target_bir_lowering=False, num_devices=1)
    arrays, args = {}, []
    for name in _INS:
        a = _np.ascontiguousarray(inputs[name])
        arrays[f"in_{name}_dram"] = a
        args.append(nc.dram_tensor(f"in_{name}_dram", a.shape, _mybir.dt.from_np(a.dtype), kind="ExternalInput").ap())
    for i, (shape, dtype) in enumerate(_OUTS):
        dt = _mybir.dt.from_np(_np.dtype(dtype))
        args.append(nc.dram_tensor(f"out_{i}_dram", shape, dt, kind="ExternalOutput").ap())
    decoder_layer(nc, *args)
    r = _run(nc, [arrays], core_ids=[0])
    got = tuple(r.results[0][f"out_{i}_dram"] for i in range(len(_OUTS)))
    return got[0]
```

```python
from contextlib import ExitStack

import concourse.bass as bass
from concourse import mybir

F32 = mybir.dt.float32
BF16 = mybir.dt.bfloat16
U32 = mybir.dt.uint32
I32 = mybir.dt.int32
ALU = mybir.AluOpType
ACT = mybir.ActivationFunctionType
AX = mybir.AxisListType

P = 128
B, S, D = 2, 1024, 256
TPB = S // P
NT = B * TPB
TOK = B * S
CC = D // P
H, DH = 16, 16
SCALE = DH ** -0.5
RES, TAPS, NF = 128, 101, 4
LINE = 2 * S
SLAB = S + (TPB - 1) * P
XH, XD = 16, 64
KV, DC = 64, 192
XSCALE = XD ** -0.5
HKV = XH * KV
NK = XH * XD // P
E, SUB = 8, 64
NM = E * SUB // P
KSEL = S // 2
LN_EPS, DEN_EPS = 1e-5, 1e-6

SHIFT_ROW = 6 * DH
STACK = SHIFT_ROW + 1
AHEAD = 5
UNITS = 4
STEPS = H // 2
TILES = UNITS * TPB
FACTOR_TILES = 2
ESLAB = S + (FACTOR_TILES - 1) * P
ASLAB = SLAB - FACTOR_TILES * P
LEAST_SUM = 2.0 ** -100
LOW_SUM = 2.0 ** -80
HALF = TPB // 2
FPOS = 1
BANKS = 8
XBUF = 5
SUMS_AT, FIN_AT, TURN_AT = 2, 3, 5
UMARGIN = 1.05

Q_RUNS = ((0, 1, 3, 0), (3, 1, 2, 0), (5, 0, 1, 0))
K_RUNS = ((0, 0, 3, 0), (3, 0, 2, 1), (5, 0, 1, 2))
LOADS = len(Q_RUNS) + len(K_RUNS)


class Counter:

    def __init__(self, eng, sem):
        self.eng, self.sem, self.n = eng, sem, 0

    def __call__(self, ins):
        self.n += 1
        ins.then_inc(self.sem, 1)
        self.eng.wait_ge(self.sem, self.n)


def decoder_layer(nc, x, ctx_in, w_qkv, w_o, w_pos, coeffs, xw_q, xw_k, xw_v, xw_o, xb_o,
                  gate_w, gate_b, ffn_w1, ffn_b1, ffn_w2, ffn_b2, out):
    with ExitStack() as stack:
        def sb(name, shape, dt=F32):
            return stack.enter_context(nc.sbuf_tensor(name, shape, dt))

        def sem(name):
            return stack.enter_context(nc.semaphore(name))

        ps = stack.enter_context(nc.psum_tensor("ps", [P, BANKS, 512], F32))

        xt = sb("xt", [P, NT, D])
        xn = sb("xn", [P, 2, 4, D])
        lnT = sb("lnT", [P, CC, TOK])
        o_all = sb("o_all", [P, NT, (H + 1) * DH])
        lnTr = o_all[:, :, :].rearrange("p a b -> p (a b)")[:, 0:CC * TOK].rearrange("p (c t) -> p c t", c=CC)
        big = sb("big", [P, NT * H * 32])
        v_all = big[:, :].rearrange("p (t h d) -> p t h d", t=NT, h=H)
        hid = big[:, :].rearrange("p (m t) -> p m t", m=NM)
        ring = sb("ring", [P, TPB, S])
        side = sb("side", [P, 7936])
        v_st = sb("v_st", [P, UNITS, TPB, 32])
        o_sb = sb("o_sb", [P, 2, D])
        wT = sb("wT", [P, CC, 3 * D])
        woT = sb("woT", [P, CC, D])
        xa = sb("xa", [P, CC, B, HKV])
        xvw = sb("xvw", [P, B, NK, D])
        ident = sb("ident", [P, P])
        anti = sb("anti", [P, P])
        ones = sb("ones", [P, P])
        bo_bc = sb("bo_bc", [P, D])
        st = sb("st", [P, 4, 6])
        mv = sb("mv", [P, 4, 2])
        ln_s = sb("ln_s", [P, 4, 4])
        rs = sb("rs", [P, 2, 4])
        sums_ = sb("sums_", [P, 2, 4])
        low = sb("low", [P, 2, 4])
        head_s = sb("head_s", [H, 8])
        x_s = sb("x_s", [P, 2, 8, XH])
        m16 = sb("m16", [P, NT])
        worst = sb("worst", [P, 2])
        general = sb("general", [1, 1], I32)
        b2p = sb("b2p", [P, B, D], BF16)
        mx = sb("mx", [P, TPB])
        mx_p = sb("mx_p", [P, 2, TPB], BF16)
        b1_sb = sb("b1_sb", [P, NM])
        gb_bc = sb("gb_bc", [P, E])
        gw_sb = sb("gw_sb", [P, CC, 32])
        r_s = sb("r_s", [P, 16])

        def cut(region, at, shape, dt=F32):
            n = 1
            for s in shape[1:]:
                n *= s
            n = n * (2 if dt == BF16 else 4) // 4
            v = region[0:shape[0], at:at + n]
            if dt != F32:
                v = v.bitcast(dt)
            if len(shape) == 3:
                v = v.rearrange("p (a b) -> p a b", b=shape[2])
            if len(shape) == 4:
                v = v.rearrange("p (a b c) -> p a b c", b=shape[2], c=shape[3])
            return v, at + n

        ring_f = ring[:, :, :].rearrange("p a b -> p (a b)")
        xvw_f = xvw[:, :, :, :].rearrange("p a b c -> p (a b c)")
        onehot, at = cut(ring_f, 0, [P, LINE])
        parts_q, at = cut(ring_f, at, [P, 2, 3, TOK], BF16)
        line_sb, at = cut(ring_f, 0, [P, 512])
        eline_sb, at = cut(ring_f, at, [P, 512])
        bound_sb, _ = cut(ring_f, at, [H, TOK], BF16)
        w_nat, at = cut(xvw_f, 0, [P, 6, D])
        wo_nat, at = cut(xvw_f, at, [P, CC, D])
        wq_nat, at = cut(big, 0, [P, CC, XH * XD])
        wqT, at = cut(big, at, [P, NK, D])
        wk_nat, at = cut(big, at, [P, 2, XH * XD])
        wv_nat, at = cut(big, at, [P, 2, XH * XD])
        xwo, at = cut(side, 0, [P, NK, D])
        kbd, at = cut(side, at, [P, B * NK, P])
        vbd, at = cut(side, at, [P, B * NK, P])
        parts_k, _ = cut(side, 0, [P, 2, 3, TOK], BF16)
        parts = (parts_q, parts_k)
        ctx_nat, at = cut(side, at, [P, DC])
        ctxT, at = cut(side, at, [P, 2, P])
        ramp, at = cut(side, at, [TAPS, RES])
        ceff, at = cut(side, at, [TAPS, H])
        bias_h, at = cut(side, at, [H, RES])
        biasT, at = cut(side, at, [RES, 32])
        coef_sb, at = cut(side, at, [NF, TAPS])
        wposT, at = cut(side, at, [NF, H])
        norm_sel, at = cut(side, at, [P, 2, 32], BF16)
        assert at <= 7936
        v_st_f = v_st[:, :, :, :].rearrange("p a b c -> p (a b c)")
        o_sb_f = o_sb[:, :, :].rearrange("p a b -> p (a b)")
        sq, _ = cut(v_st_f, 0, [P, 4, 512], BF16)
        resid, _ = cut(xn[:, :, :, :].rearrange("p a b c -> p (a b c)"), 0, [P, 4, 512])
        slab = side[:, 0:2 * ASLAB].rearrange("p (a b) -> p a b", a=2)
        st_q = side[:, 2 * ASLAB:2 * ASLAB + 4 * 512].bitcast(BF16).rearrange("p (a b) -> p a b", a=UNITS)
        st_k = side[:, 2 * ASLAB + 4 * 512:2 * ASLAB + 8 * 512].bitcast(BF16).rearrange("p (a b) -> p a b", a=UNITS)
        eslab, _ = cut(lnT[:, :, :].rearrange("p a b -> p (a b)"), 0, [P, 2, ESLAB])
        slab_g = side[:, 0:SLAB]
        xp, at = cut(ring_f, 0, [P, XBUF, HKV])
        xpT, at = cut(ring_f, at, [P, 3, HKV])
        b2x1, at = cut(v_st_f, 0, [P, B, D])
        b2x2, at = cut(v_st_f, at, [P, B, D])
        b2_round, _ = cut(o_sb_f, 0, [P, B, D], BF16)
        w1, at = cut(side, 0, [P, CC, E * SUB])
        w2, at = cut(side, at, [P, NM, D])
        b2x, at = cut(side, at, [P, B, D])
        pick, at = cut(side, at, [P, B * NM, P], BF16)
        sel_b, at = cut(side, at, [P, S], BF16)
        block8, at = cut(side, at, [P, P], BF16)
        digits, at = cut(side, at, [P, 10], U32)
        gates, at = cut(side, at, [P, 4, NT * E])
        expw, at = cut(side, at, [P, E])
        assert at <= 7936
        gT, at = cut(ring_f, 0, [P, 512])
        rrep, at = cut(ring_f, at, [P, TPB, P])
        rr, at = cut(ring_f, at, [P, S])
        junk, at = cut(ring_f, at, [P, S])
        above, at = cut(ring_f, at, [P, S])
        prefix, at = cut(ring_f, at, [P, S])
        o_out, _ = cut(xn[:, :, :, :].rearrange("p a b c -> p (a b c)"), 0, [P, 4, 2 * D])

        d_q = nc.dram_tensor("d_q", (3, H * DH, TOK), BF16, kind="Internal").ap()
        d_k = nc.dram_tensor("d_k", (3, H * DH, TOK), BF16, kind="Internal").ap()
        d_bound = nc.dram_tensor("d_bound", (H, TOK), BF16, kind="Internal").ap()
        d_line = nc.dram_tensor("d_line", (H, LINE), F32, kind="Internal").ap()
        d_max = nc.dram_tensor("d_max", (2, S), BF16, kind="Internal").ap()
        d_eline = nc.dram_tensor("d_eline", (H, LINE), F32, kind="Internal").ap()

        small_in, x_in = sem("small_in"), [sem(f"x_in{g}") for g in range(4)]
        w_in, xw_in, wq_in, xwo_in, ffn_in = sem("w_in"), sem("xw_in"), sem("wq_in"), sem("xwo_in"), sem("ffn_in")
        const_ready, gw_zeroed, gate_in = sem("const_ready"), sem("gw_zeroed"), sem("gate_in")
        dve_step, act_step, pool_step = sem("dve_step"), sem("act_step"), sem("pool_step")
        job_done, act_took, dve_took = sem("job_done"), sem("act_took"), sem("dve_took")
        ln_done = sem("ln_done")
        part1_done, resid_done, part2_done, sq_done, part3_done = (
            sem("part1_done"), sem("resid_done"), sem("part2_done"), sem("sq_done"), sem("part3_done"))
        kparts_out, qparts_out, line_out, bound_out = sem("kparts_out"), sem("qparts_out"), sem("line_out"), sem("bound_out")
        kmax_done, v_zeroed = sem("kmax_done"), sem("v_zeroed")
        EXP_LINE = 8
        stack_in = [sem(f"stack_in{u}") for u in range(UNITS)]
        slab_in = [sem(f"slab_in{h}") for h in range(2)]
        eslab_in = [sem(f"eslab_in{h}") for h in range(2)]
        qk_done, add_done, exp_done, fexp_done, factor_done, pv_done = (
            sem("qk_done"), sem("add_done"), sem("exp_done"), sem("fexp_done"), sem("factor_done"), sem("pv_done"))
        heads_out, turned, finished, v_staged = sem("heads_out"), sem("turned"), sem("finished"), sem("v_staged")
        attn_step, load_go, stage_go = sem("attn_step"), sem("load_go"), sem("stage_go")
        bo_added, centred, xexp_done, xrecip_done, xprob_done = (
            sem("bo_added"), sem("centred"), sem("xexp_done"), sem("xrecip_done"), sem("xprob_done"))
        rrep_done, digit_asked, chosen, out_done = sem("rrep_done"), sem("digit_asked"), sem("chosen"), sem("out_done")
        worst_done, worst_turned, general_known = sem("worst_done"), sem("worst_turned"), sem("general_known")
        g_rows, g_in, g_v, g_qk, g_add, g_max, g_maxout, g_row, g_exp, g_pv, g_heads, g_turned, g_fin, g_step = (
            sem(f"general_{n}") for n in "rows in v qk add max maxout row exp pv heads turned fin step".split())
        stored = [sem(f"stored{i}") for i in range(4)]
        b2_ready = sem("b2_ready")
        ffn_const, gcentred, gexp_done = sem("ffn_const"), sem("gcentred"), sem("gexp_done")

        jobs = []

        def turns(name, g):
            return [(name, (g, c), "act") for c in range(CC)]

        jobs += [("wT", n, "act") for n in range(3)] + [("woT", 0, "act")]
        for g in range(4):
            jobs += turns("lnT", g) + turns("lnTr", g)
            jobs += {0: [("ctxT", 0, "act")],
                     1: [("ceff", 0, "dve"), ("kT", 0, "act"), ("bias", 0, "dve"), ("kT", 1, "act"), ("biasT", 0, "dve"),
                         ("vT", 0, "dve"), ("line", 0, "dve"), ("vT", 1, "dve")],
                     2: [("wqT", n, "act") for n in range(4)] + [("xa", n, "act") for n in range(4)],
                     3: [("xa", n, "act") for n in range(4, 8)] + [("xvw", n, "dve") for n in range(8)]}[g]
        proj_order = [(half, n, e) for half in (1, 0) for n in range(4) for e in range(2)]
        for i, (half, n, e) in enumerate(proj_order):
            jobs.append(("proj", (half, n, e), "dve"))
            if e == 1 and i > 1:
                jobs.append(("norm", i // 2 - 1, "dve" if i // 2 - 1 < 4 else "act"))
        jobs.append(("norm", 7, "act"))
        jobs += [("v", n, "act") for n in range(NT // 2)]

        TURN_LAG, OUT_LAG = 3, 4
        plan = [("wo", 0), ("norm2", 0), ("wo", 1), ("wo", 2), ("norm2T", 0), ("norm2", 1), ("wo", 3), ("norm2T", 1)]
        extras = {4: [("norm2", 2)], 6: [("norm2T", 2)], 7: [("norm2", 3)], 8: [("norm2T", 3), ("norm3", 0)],
                  9: [("norm3T", 0)], 11: [("norm3", 1)], 13: [("norm3T", 1)], 15: [("norm3", 2)], 17: [("norm3T", 2)]}
        for t in range(NT + OUT_LAG):
            if t < NT:
                plan.append(("logits", t))
            if TURN_LAG <= t < NT + TURN_LAG:
                plan.append(("probs", t - TURN_LAG))
            if t >= OUT_LAG:
                plan.append(("out", t - OUT_LAG))
            plan += extras.get(t, [])
        plan += [("norm3", 3), ("norm3T", 3)]
        ln_order = [("norm1", g) for g in range(4)] + [k for k in plan if k in [(f"norm{i}", g) for i in (2, 3) for g in range(4)]]
        for kind, k in plan:
            if kind == "wo":
                jobs += turns("oT", k) + [("wo", 2 * k + i, "dve") for i in range(2)]
            elif kind in ("norm2T", "norm3T"):
                jobs += turns(kind, k)
            elif kind == "logits":
                jobs += [("xl", (k, hf), "dve") for hf in range(2)]
            elif kind == "probs":
                jobs += [("xpT", (k, hf), "act") for hf in range(2)]
            elif kind == "out":
                jobs += [("xo", k, "dve")]
        jobs += [("gate", 0, "act"), ("gateT", 0, "dve")]
        w1_order = [(m, n) for n in range(4) for m in range(NM)]
        W1_EARLY = 4
        jobs += [("w1", k, "act") for k in w1_order[:W1_EARLY]]
        jobs += [("rrep", 0, "dve"), ("rrep", 1, "act")]
        for i in range(10):
            jobs += [("digit", i, "dve"), ("w1", w1_order[W1_EARLY + i], "act")]
        jobs += [("w1", k, "act") for k in w1_order[W1_EARLY + 10:]]
        for n in range(4):
            jobs += [("mask", (m, n), "dve") for m in range(NM)]
            if n:
                jobs += [("w2", t, "dve") for t in range(4 * n - 4, 4 * n)]
        jobs += [("w2", t, "dve") for t in range(12, NT)]
        index = {(name, key): j for j, (name, key, _) in enumerate(jobs)}
        took = {"act": act_took, "dve": dve_took}

        def taken(eng, j):
            who = jobs[j][2]
            eng.wait_ge(took[who], sum(k[2] == who for k in jobs[:j + 1]))

        def bank(j):
            return ps[:, j % BANKS, :]

        def job(pe, name, key):
            j = index[name, key]
            if j >= BANKS:
                taken(pe, j - BANKS)
            return bank(j)

        def result(eng, name, key):
            j = index[name, key]
            eng.wait_ge(job_done, j + 1)
            return bank(j)

        def after(eng, name, key):
            eng.wait_ge(job_done, index[name, key] + 1)

        lnr_at = [(g // 2) * S + 512 * (1 - g % 2) for g in range(4)]

        slot_of = [g % 3 for g in range(TILES)]
        pv_pos = [h + k for h in range(0, TILES, HALF) for k in (0, 2, 3, FPOS)]
        rank = {g: i for i, g in enumerate(pv_pos)}
        FACTORS, ADDS = TILES // HALF, TILES - TILES // HALF

        key_tile = [(2, 0, 3, 4, 5, 1, 6, 7)[g % TPB] for g in range(TILES)]

        def is_factor(g):
            return g % HALF == FPOS

        def factors_to(g):
            return (g + HALF - FPOS) // HALF

        def slot_before(g):
            k = g - 1
            while slot_of[k % TILES] != slot_of[g % TILES]:
                k -= 1
            return k

        def read_out(eng, it, g):
            if is_factor(g):
                eng.wait_ge(fexp_done, it * FACTORS + factors_to(g))
            else:
                eng.wait_ge(add_done, it * ADDS + (g + 1 - factors_to(g)))

        def ring_free(eng, it, g):
            eng.wait_ge(pv_done, it * TILES + rank[g] + 1)

        block = stack.enter_context(nc.Block())

        @block.sync
        def _(sp):
            for g in range(4):
                sp.dma_start(xt[:, 4 * g:4 * g + 4, :],
                             x.rearrange("b (t p) c -> p (b t) c", p=P)[:, 4 * g:4 * g + 4, :]).then_inc(x_in[g], 16)
                if g == 0:
                    sp.dma_start(w_nat, w_qkv.rearrange("(a p) c -> p a c", p=P)).then_inc(w_in, 16)
                    sp.dma_start(wo_nat, w_o.rearrange("(a p) c -> p a c", p=P)).then_inc(w_in, 16)
            for w_sb, w in ((wk_nat, xw_k), (wv_nat, xw_v)):
                sp.dma_start(w_sb[:, 0, :], w[0:P, :]).then_inc(xw_in, 16)
                sp.dma_start(w_sb[0:DC - P, 1, :], w[P:DC, :]).then_inc(xw_in, 16)
            sp.dma_start(wq_nat, xw_q.rearrange("(a p) n -> p a n", p=P)).then_inc(wq_in, 16)
            sp.dma_start(xwo, xw_o.rearrange("(k p) n -> p k n", p=P)).then_inc(xwo_in, 16)
            taken(sp, index["line", 0])
            for n in range(4):
                sp.dma_start(d_line[:, n * 512:(n + 1) * 512], line_sb[32 * n:32 * n + H, :]).then_inc(line_out, 16)
            sp.wait_ge(act_step, EXP_LINE)
            for n in range(4):
                sp.dma_start(d_eline[:, n * 512:(n + 1) * 512], eline_sb[32 * n:32 * n + H, :]).then_inc(line_out, 16)
            for i, (half, n, e) in enumerate(proj_order):
                sp.wait_ge(part3_done, i + 1)
                sp.dma_start((d_q, d_k)[half][:, e * P:(e + 1) * P, n * 512:(n + 1) * 512].rearrange("r q t -> q r t"),
                             parts[half][:, e, :, n * 512:(n + 1) * 512]).then_inc(kparts_out if half else qparts_out, 16)
            taken(sp, index["norm", 7])
            sp.dma_start(d_bound, bound_sb).then_inc(bound_out, 16)
            sp.wait_ge(line_out, 16 * 8)
            sp.wait_ge(kparts_out, 16 * 8)
            sp.wait_ge(qparts_out, 16 * 8)
            sp.wait_ge(bound_out, 16)

            def load_products(head, u, b, done):
                for dst, src, runs in ((st_q, d_q, Q_RUNS), (st_k, d_k, K_RUNS)):
                    for row, step, n, part in runs:
                        v = bass.AP(tensor=src.tensor, offset=head * (DH * TOK) + (b * S + part * H * DH * TOK),
                                    ap=[[step * H * DH * TOK, n], [TOK, DH], [1, S]])
                        sp.dma_start(dst[row * DH:(row + n) * DH, u, :], v).then_inc(done, 16)

            def load_stack(head, u):
                load_products(head, u, u % 2, stack_in[u])
                v = bass.AP(tensor=d_bound.tensor, offset=head * TOK + (u % 2) * S, ap=[[TOK, 1], [1, S]])
                sp.dma_start(st_q[SHIFT_ROW:STACK, u, :], v).then_inc(stack_in[u], 16)

            def load_slab(dst, src, head, at, n, done):
                v = bass.AP(tensor=src.tensor, offset=head * LINE + at, ap=[[1, P], [1, n]])
                sp.dma_start(dst, v).then_inc(done, 16)

            for u in range(UNITS):
                load_stack(u // 2, u)
                if u % 2 == 0:
                    load_slab(slab[:, u // 2, :], d_line, u // 2, FACTOR_TILES * P, ASLAB, slab_in[u // 2])
                    load_slab(eslab[:, u // 2, :], d_eline, u // 2, 0, ESLAB, eslab_in[u // 2])
            with sp.Fori(0, STEPS - 1) as it:
                for u in range(UNITS):
                    sp.wait_ge(qk_done, it * TILES + TPB * (u + 1))
                    load_stack(it * 2 + 2 + u // 2, u)
                    if u % 2 == 1:
                        sp.wait_ge(add_done, it * ADDS + ADDS // UNITS * (u + 1))
                        load_slab(slab[:, u // 2, :], d_line, it * 2 + 2 + u // 2, FACTOR_TILES * P, ASLAB, slab_in[u // 2])
                        sp.wait_ge(factor_done, it * FACTORS + FACTORS // UNITS * (u + 1))
                        sp.sem_inc(load_go, 1)
                        load_slab(eslab[:, u // 2, :], d_eline, it * 2 + 2 + u // 2, 0, ESLAB, eslab_in[u // 2])

            sp.wait_ge(general_known, 1)
            with sp.If(sp.value_load(general[0:1, 0:1], min_val=0, max_val=1) > 0):
                with sp.Fori(0, H) as h:
                    for b in range(B):
                        n = h * B + (b + 1)
                        sp.wait_ge(g_fin, n)
                        load_products(h, 0, b, g_in)
                        load_slab(slab_g, d_line, h, 0, SLAB, g_in)
                        sp.wait_ge(g_max, n)
                        with nc.allow_non_contiguous_dma("a column of maxima to a row"):
                            sp.dma_start(d_max.rearrange("a (t p) -> p a t", p=P), mx_p[:, :, :]).then_inc(g_maxout, 16)
                        sp.wait_ge(g_maxout, n * 16)
                        sp.dma_start(st_q[SHIFT_ROW:SHIFT_ROW + 2, 0, :], d_max).then_inc(g_row, 16)
                sp.wait_ge(g_fin, H * B + 1)

            sp.wait_ge(ffn_const, 1)
            for c in range(CC):
                sp.dma_start(w1[:, c, :].rearrange("p (e h) -> p e h", e=E),
                             ffn_w1[:, c * P:(c + 1) * P, :].rearrange("e p h -> p e h")).then_inc(ffn_in, 16)
            sp.dma_start(w2, ffn_w2.rearrange("(m a) h d -> (a h) m d", a=2)).then_inc(ffn_in, 16)
            for c, copy in enumerate((b2x, b2x1, b2x2)):
                for b in range(B):
                    sp.dma_start(copy[b * 64 + c:b * 64 + c + 57:8, b, :], ffn_b2).then_inc(ffn_in, 16)
            for t in range(NT):
                sp.wait_ge(out_done, t + 1)
                sp.dma_start(out.rearrange("b (t p) c -> (b t) p c", p=P)[t], o_out[:, t % 4, 0:D]).then_inc(stored[t % 4], 16)
            for i in range(4):
                sp.wait_ge(stored[i], 16 * (NT // 4))

        @block.gpsimd
        def _(pool):
            step = Counter(pool, pool_step)
            for m in (ident, anti):
                step(pool.memset(m[:, :], 0.0))
            step(pool.affine_select(out=ident[:, :], in_=ident[:, :], compare_op=ALU.not_equal, fill=1.0,
                                    base=0, pattern=[[-1, P]], channel_multiplier=1))
            pool.sem_inc(const_ready, 1)
            step(pool.affine_select(out=anti[:, :], in_=anti[:, :], compare_op=ALU.not_equal, fill=1.0,
                                    base=1 - P, pattern=[[1, P]], channel_multiplier=1))
            pool.sem_inc(const_ready, 1)
            step(pool.iota(ramp, pattern=[[1, RES]], base=0, channel_multiplier=-1, allow_small_or_imprecise_dtypes=True))
            step(pool.tensor_scalar(ramp, ramp, 0.0, None, ALU.max))
            step(pool.tensor_scalar(ramp, ramp, 1.0 / (RES - 1), None, ALU.mult))
            step(pool.memset(biasT, 0.0))
            step(pool.memset(onehot, 1.0))
            for at, base, way in ((0, (RES - 1) * (S - 1), -1), (S, RES - 1, 1)):
                part = onehot[:, at:at + S]
                step(pool.affine_select(out=part, in_=part, compare_op=ALU.is_ge, fill=0.0, base=base + (S - 1) // 2,
                                        pattern=[[way * (RES - 1), S]], channel_multiplier=-(S - 1)))
                step(pool.affine_select(out=part, in_=part, compare_op=ALU.is_ge, fill=0.0, base=(S - 1) // 2 - base,
                                        pattern=[[-way * (RES - 1), S]], channel_multiplier=S - 1))
            pool.sem_inc(const_ready, 1)
            step(pool.memset(kbd, 0.0))
            step(pool.memset(vbd, 0.0))
            pool.sem_inc(const_ready, 1)
            step(pool.memset(norm_sel, 1.0))
            for e in range(2):
                part = norm_sel[:, e, :]
                step(pool.affine_select(out=part, in_=part, compare_op=ALU.is_ge, fill=0.0, base=P * e,
                                        pattern=[[-DH, 32]], channel_multiplier=1))
                step(pool.affine_select(out=part, in_=part, compare_op=ALU.is_ge, fill=0.0, base=DH - 1 - P * e,
                                        pattern=[[DH, 32]], channel_multiplier=-1))
            step(pool.memset(gw_sb[:, :, :], 0.0))
            step(pool.memset(ones[:, :], 1.0))
            pool.sem_inc(const_ready, 1)
            after(pool, "xa", 7)
            after(pool, "vT", 1)
            step(pool.memset(v_all[:, :, :, DH:32], 0.0))
            pool.memset(v_all[:, :, :, DH:DH + 1], 1.0).then_inc(v_zeroed, 1)
            for i, (half, n, e) in enumerate(proj_order):
                taken(pool, index["proj", (half, n, e)])
                pool.wait_ge(part2_done, i + 1)
                p_ = parts[half][:, e, :, n * 512:(n + 1) * 512]
                pool.tensor_tensor(p_[:, 2, :], resid[:, i % 4, :], p_[:, 1, :], ALU.subtract).then_inc(part3_done, 1)
            pool.wait_ge(v_zeroed, 1)
            after(pool, "norm", 7)
            pool.wait_ge(kparts_out, 16 * 8)
            pool.wait_ge(part3_done, 16)
            step(pool.memset(st_k[SHIFT_ROW:STACK, :, :], -1.0))
            pool.sem_inc(const_ready, 1)

            def stage(head, u):
                b = u % 2
                return pool.tensor_copy(v_st[:, u, :, :], v_all[:, b * TPB:(b + 1) * TPB, :, :].rearrange(
                    "p t h d -> p t (h d)")[:, :, bass.ds(head * 32, 32)])

            taken(pool, index["v", NT // 2 - 1])
            for u in range(UNITS - 1):
                stage(u // 2, u).then_inc(v_staged, 1)

            def attention(it, last=False):
                for k in range(FACTORS):
                    g, u = k * HALF + FPOS, k * HALF // TPB
                    if k % 4 == 0:
                        pool.wait_ge(eslab_in[u // 2], it * 16 + 16)
                    pool.wait_ge(fexp_done, it * FACTORS + (k + 1))
                    r_ = ring[:, g % TPB, :]
                    jt = key_tile[g]
                    pool.tensor_tensor(r_, r_, eslab[:, u // 2, jt * P:jt * P + S], ALU.mult).then_inc(factor_done, 1)
                    if k % 2 == 0 and (u == 0 or not last):
                        pool.wait_ge(pv_done, it * TILES + TPB * (u + 1))
                        pool.sem_inc(stage_go, 1)
                        stage(it * 2 + (1 if u == 0 else 2 + (u - 1) // 2), (u - 1) % UNITS).then_inc(v_staged, 1)

            with pool.Fori(0, STEPS - 1) as it:
                attention(it)
            attention(STEPS - 1, last=True)

            pool.wait_ge(general_known, 1)
            with pool.If(pool.value_load(general[0:1, 0:1], min_val=0, max_val=1) > 0):
                pool.wait_ge(factor_done, STEPS * FACTORS)
                pool.memset(st_k[SHIFT_ROW:SHIFT_ROW + 2, 0, :], -1.0).then_inc(g_rows, 1)
                pool.wait_ge(g_rows, 1)
                with pool.Fori(0, H) as h:
                    for b in range(B):
                        pool.wait_ge(g_fin, h * B + (b + 1))
                        pool.sem_inc(stage_go, 1)
                        pool.tensor_copy(v_st[:, 0, :, :], v_all[:, b * TPB:(b + 1) * TPB, :, :].rearrange(
                            "p t h d -> p t (h d)")[:, :, bass.ds(h * 32, 32)]).then_inc(g_v, 1)
                pool.wait_ge(g_fin, H * B + 1)

            for copy in (b2x, b2x1, b2x2):
                step(pool.memset(copy, 0.0))
            step(pool.memset(pick, 1.0))
            for b in range(B):
                for m in range(NM):
                    for a in range(2):
                        part = pick[:, b * NM + m, a * SUB:(a + 1) * SUB]
                        row = b * 64 + (2 * m + a) * 8
                        step(pool.affine_select(out=part, in_=part, compare_op=ALU.is_equal, fill=0.0, base=-row,
                                                pattern=[[0, SUB]], channel_multiplier=1))
            step(pool.memset(block8, 1.0))
            blk = block8.rearrange("p (g c) -> p g c", c=8)
            step(pool.affine_select(out=blk, in_=blk, compare_op=ALU.is_ge, fill=0.0, base=0,
                                    pattern=[[-8, 16], [0, 8]], channel_multiplier=1))
            step(pool.affine_select(out=blk, in_=blk, compare_op=ALU.is_ge, fill=0.0, base=7,
                                    pattern=[[8, 16], [0, 8]], channel_multiplier=-1))
            step(pool.iota(expw, pattern=[[-1, E]], base=E, channel_multiplier=0, allow_small_or_imprecise_dtypes=True))
            step(pool.iota(r_s[:, 12:13].bitcast(I32), pattern=[[0, 1]], base=0, channel_multiplier=1))
            pool.sem_inc(ffn_const, 1)
            for kind, k in plan:
                if kind == "norm2":
                    pool.wait_ge(ln_done, ln_order.index((kind, k)) + 1)
                    pool.tensor_tensor(xt[:, 4 * k:4 * k + 4, :], xt[:, 4 * k:4 * k + 4, :],
                                       bo_bc[:, :].unsqueeze(1).broadcast_to([P, 4, D]), ALU.add).then_inc(bo_added, 1)
                elif kind == "logits":
                    pool.wait_ge(xrecip_done, k + 1)
                    v = xp[:, k % XBUF, :].rearrange("p (h k) -> p h k", h=XH)
                    pool.tensor_tensor(v, v, x_s[:, 1, k % 8, :].unsqueeze(2).broadcast_to([P, XH, KV]),
                                       ALU.mult).then_inc(xprob_done, 1)
                    if k == 4:
                        pool.wait_ge(ffn_in, 16 * 9)
                        step(pool.tensor_copy(b2_round, b2x1))
                    elif k == 5:
                        step(pool.tensor_tensor(b2x1, b2x1, b2_round, ALU.subtract))
                    elif k in (6, 8):
                        step(pool.tensor_copy(b2_round, b2x2))
                    elif k in (7, 9):
                        step(pool.tensor_tensor(b2x2, b2x2, b2_round, ALU.subtract))
                    elif k == 10:
                        step(pool.tensor_tensor(b2x1, b2x1, b2x, ALU.add))
                    elif k == 11:
                        step(pool.tensor_tensor(b2x1, b2x1, b2x2, ALU.add))
                    elif k == 12:
                        pool.tensor_copy(b2p[:, :, :], b2x1).then_inc(b2_ready, 1)

        @block.scalar
        def _(act):
            act.dma_start(coef_sb, coeffs).then_inc(small_in, 16)
            with nc.allow_non_contiguous_dma("64 elements"):
                act.dma_start(wposT, w_pos.rearrange("h f -> f h")).then_inc(small_in, 16)
                act.dma_start(b1_sb[:, :], ffn_b1.rearrange("(m a) h -> (a h) m", a=2)).then_inc(small_in, 16)
            act.dma_start(ctx_nat, ctx_in.rearrange("b k c -> (b k) c")).then_inc(small_in, 16)
            act.dma_start(bo_bc[:, :], xb_o.rearrange("(a c) -> a c", a=1).broadcast_to([P, D])).then_inc(small_in, 16)
            act.dma_start(gb_bc[:, :], gate_b.rearrange("(a c) -> a c", a=1).broadcast_to([P, E])).then_inc(small_in, 16)

            def copy(name, key, dst, **kw):
                act.activation(dst, result(act, name, key), ACT.Copy, **kw).then_inc(act_took, 1)

            def turned_group(name, g):
                for c in range(CC):
                    copy(name, (g, c), lnT[:, c, g * 512:(g + 1) * 512])

            def both_ways(g):
                turned_group("lnT", g)
                for c in range(CC):
                    copy("lnTr", (g, c), lnTr[:, c, lnr_at[g]:lnr_at[g] + 512])

            wT_f = wT[:, :, :].rearrange("p a b -> p (a b)")
            for n in range(3):
                copy("wT", n, wT_f[:, n * 512:(n + 1) * 512])
            copy("woT", 0, woT[:, :, :].rearrange("p a b -> p (a b)"))
            both_ways(0)
            b_ = result(act, "ctxT", 0)
            act.activation(ctxT[:, 0, :], b_[:, 0:P], ACT.Copy).then_inc(act_step, 1)
            act.activation(ctxT[0:DC - P, 1, :], b_[0:DC - P, P:2 * P], ACT.Copy).then_inc(act_took, 1)
            both_ways(1)
            act.wait_ge(const_ready, 4)
            for n in range(2):
                b_ = result(act, "kT", n)
                for hl in range(2):
                    rows = slice(64 * hl, 64 * hl + 64)
                    for b in range(B):
                        ins = act.activation(kbd[rows, b * NK + 4 * n:b * NK + 4 * n + 4, 64 * hl:64 * hl + 64],
                                             b_[rows, :].rearrange("p (k c) -> p k c", k=4)[:, :, b * KV:(b + 1) * KV],
                                             ACT.Copy)
                        ins.then_inc(act_took if hl and b else act_step, 1)
            both_ways(2)
            taken(act, index["line", 0])
            act.activation(eline_sb, line_sb, ACT.Exp).then_inc(act_step, 1)
            wqT_f = wqT.rearrange("p a b -> p (a b)")
            for n in range(4):
                copy("wqT", n, wqT_f[:, n * 512:(n + 1) * 512])
            xa_f = xa[:, :, :, :].rearrange("p c b n -> p (c b n)")
            for n in range(8):
                if n == 4:
                    both_ways(3)
                copy("xa", n, xa_f[:, n * 512:(n + 1) * 512])
            act.wait_ge(const_ready, 5)
            act.dma_start(gw_sb[:, :, 0:E], gate_w.rearrange("(c p) e -> p c e", p=P)).then_inc(gate_in, 16)

            def second_part(i):
                half, n, e = proj_order[i]
                taken(act, index["proj", (half, n, e)])
                act.activation(parts[half][:, e, 1, n * 512:(n + 1) * 512], resid[:, i % 4, :], ACT.Copy).then_inc(part2_done, 1)

            def bound(n):
                b_ = result(act, "norm", 4 + n)
                if n == 0:
                    act.wait_ge(kmax_done, 1)
                act.activation(bound_sb[:, n * 512:(n + 1) * 512], b_[0:H, :], ACT.Sqrt,
                               scale=head_s[:, 4 + n // 2:5 + n // 2]).then_inc(act_took, 1)

            for i, (half, n, e) in enumerate(proj_order):
                act.activation(parts[half][:, e, 0, n * 512:(n + 1) * 512], result(act, "proj", (half, n, e)), ACT.Copy,
                               scale=SCALE if half == 0 else 1.0).then_inc(part1_done, 1)
                if i:
                    second_part(i - 1)
                if e == 1 and i // 2 - 1 >= 4:
                    bound(i // 2 - 5)
            second_part(15)
            bound(3)
            act.wait_ge(v_zeroed, 1)
            for n in range(NT // 2):
                act.activation(v_all[:, 2 * n:2 * n + 2, :, 0:DH],
                               result(act, "v", n).rearrange("p (t h d) -> p t h d", t=2, h=H),
                               ACT.Copy).then_inc(act_took, 1)

            def heads(o):
                return act.activation(o_sb[:, o, :], ps[:, 6 + o, 0:D], ACT.Copy).then_inc(heads_out, 1)

            with act.Fori(0, STEPS) as it:
                for k in range(FACTORS):
                    g = k * HALF
                    act.wait_ge(qk_done, it * TILES + g + FPOS + 1)
                    ring_free(act, it, g + FPOS)
                    slot = slot_of[g + FPOS]
                    act.activation(ring[:, (g + FPOS) % TPB, :],
                                   ps[:, 2 * slot:2 * slot + 2, :].rearrange("p a b -> p (a b)"), ACT.Exp).then_inc(fexp_done, 1)
                    for first in (g, g + 2, g + 3):
                        act.wait_ge(add_done, it * ADDS + (first + 1 - factors_to(first)))
                        r_ = ring[:, first % TPB, :]
                        act.activation(r_, r_, ACT.Exp).then_inc(exp_done, 1)
                    if k % 2 == 0:
                        u = g // TPB
                        act.wait_ge(pv_done, it * TILES + TPB * (u + 1))
                        heads((u - 1) % 2)
            act.wait_ge(pv_done, (STEPS * UNITS + 1) * TPB)
            heads(1)

            act.wait_ge(general_known, 1)
            with act.If(act.value_load(general[0:1, 0:1], min_val=0, max_val=1) > 0):
                with act.Fori(0, H) as h:
                    for b in range(B):
                        for jt in range(TPB):
                            act.wait_ge(g_add, h * (B * 2 * TPB) + (b * 2 * TPB + TPB + jt + 1))
                            r_ = ring[:, jt % 2, :]
                            act.activation(r_, r_, ACT.Exp).then_inc(g_exp, 1)
                        act.wait_ge(g_pv, h * B + (b + 1))
                        act.activation(o_sb[:, 0, :], ps[:, 6, 0:D], ACT.Copy).then_inc(g_heads, 1)

            for kind, k in plan:
                if kind == "wo":
                    turned_group("oT", k)
                elif kind in ("norm2T", "norm3T"):
                    turned_group(kind, k)
                elif kind == "logits":
                    act.wait_ge(centred, 2 * k + 2)
                    v = xp[:, k % XBUF, :]
                    act.activation(v, v, ACT.Exp, scale=XSCALE).then_inc(xexp_done, 1)
                elif kind == "probs":
                    for hf in range(2):
                        copy("xpT", (k, hf), xpT[:, k % 3, hf * 512:(hf + 1) * 512])
            copy("gate", 0, gT)
            act.wait_ge(gcentred, 1)
            act.activation(gates[:, 1, :], gates[:, 0, :], ACT.Exp).then_inc(gexp_done, 1)
            for i, (m, n) in enumerate(w1_order):
                if i == W1_EARLY:
                    copy("rrep", 1, rr[:, 512:1024])
                act.activation(hid[:, m, n * 512:(n + 1) * 512], result(act, "w1", (m, n)), ACT.Gelu,
                               bias=b1_sb[:, m:m + 1]).then_inc(act_took, 1)

        @block.tensor
        def _(pe):
            def end(ins):
                ins.then_inc(job_done, 1)

            def turn4(name, key, ins_):
                b_ = job(pe, name, key)
                for src, m, at in ins_:
                    last = pe.transpose(b_[0:src.shape[1], at:at + P], src, m[:, :])
                end(last)

            def turn_norm(name, kind, g, m, back=False):
                i_ = ln_order.index((kind, g))
                pe.wait_ge(ln_done, i_ + 1)
                for c in range(CC):
                    turn4(name, (g, c), [(xn[:, i_ % 2, i, c * P:(c + 1) * P], m, (3 - i if back else i) * P)
                                         for i in range(4)])

            def cross_weights(w, name, n):
                b_ = job(pe, name, n)
                for i in range(4):
                    k = 4 * n + i
                    pe.matmul(b_[:, i * P:(i + 1) * P], w[:, 0, k * P:(k + 1) * P], ctxT[:, 0, :],
                              start=True, stop=False, skip_group_check=True)
                    last = pe.matmul(b_[:, i * P:(i + 1) * P], w[0:DC - P, 1, k * P:(k + 1) * P], ctxT[0:DC - P, 1, :],
                                     start=False, stop=True, skip_group_check=True)
                end(last)

            def cross_keys(n):
                c, b, k0 = n // 4, n // 2 % 2, 4 * (n % 2)
                b_ = job(pe, "xa", n)
                for i in range(4):
                    last = pe.matmul(b_[:, i * P:(i + 1) * P], wqT[:, k0 + i, c * P:(c + 1) * P], kbd[:, b * NK + k0 + i, :],
                                     start=True, stop=True, skip_group_check=True)
                end(last)

            pe.wait_ge(const_ready, 1)
            pe.wait_ge(w_in, 32)
            for n in range(3):
                turn4("wT", n, [(w_nat[:, (4 * n + i) % 6, ((4 * n + i) // 6) * P:((4 * n + i) // 6 + 1) * P], ident, i * P)
                                for i in range(4)])
            turn4("woT", 0, [(wo_nat[:, i % 2, (i // 2) * P:(i // 2 + 1) * P], ident, i * P) for i in range(4)])
            pe.wait_ge(const_ready, 2)
            for g in range(4):
                turn_norm("lnT", "norm1", g, ident)
                turn_norm("lnTr", "norm1", g, anti, back=True)
                if g == 0:
                    pe.wait_ge(small_in, 96)
                    turn4("ctxT", 0, [(ctx_nat[:, 0:P], ident, 0), (ctx_nat[:, P:DC], ident, P)])
                elif g == 1:
                    pe.wait_ge(const_ready, 3)
                    end(pe.matmul(job(pe, "ceff", 0)[0:TAPS, 0:H], coef_sb, wposT, start=True, stop=True))
                    pe.wait_ge(xw_in, 64)
                    taken(pe, index["ctxT", 0])
                    cross_weights(wk_nat, "kT", 0)
                    taken(pe, index["ceff", 0])
                    end(pe.matmul(job(pe, "bias", 0)[0:H, 0:RES], ceff, ramp, start=True, stop=True))
                    cross_weights(wk_nat, "kT", 1)
                    taken(pe, index["bias", 0])
                    end(pe.transpose(job(pe, "biasT", 0)[:, 0:H], bias_h, ident[0:H, 0:H]))
                    cross_weights(wv_nat, "vT", 0)
                    taken(pe, index["biasT", 0])
                    b_ = job(pe, "line", 0)
                    for n in range(4):
                        last = pe.matmul(b_[32 * n:32 * n + 32, :], biasT, onehot[:, n * 512:(n + 1) * 512],
                                         start=True, stop=True, skip_group_check=True)
                    end(last)
                    cross_weights(wv_nat, "vT", 1)
                elif g == 2:
                    pe.wait_ge(wq_in, 16)
                    for n in range(4):
                        turn4("wqT", n, [(wq_nat[:, i % 2, (2 * n + i // 2) * P:(2 * n + i // 2 + 1) * P], ident, i * P)
                                         for i in range(4)])
                    taken(pe, index["wqT", 3])
                    for n in range(4):
                        cross_keys(n)
            for n in range(4, 8):
                cross_keys(n)
            taken(pe, index["vT", 1])
            pe.wait_ge(xwo_in, 16)
            for n in range(8):
                b_ = job(pe, "xvw", n)
                for i in range(2):
                    last = pe.matmul(b_[:, i * D:(i + 1) * D], vbd[:, 2 * n + i, :], xwo[:, (2 * n + i) % NK, :],
                                     start=True, stop=True, skip_group_check=True)
                end(last)
            taken(pe, index["lnT", (3, 1)])
            taken(pe, index["lnTr", (3, 1)])
            pe.wait_ge(const_ready, 5)

            def norm(k):
                pe.wait_ge(sq_done, 2 * k + 2)
                b_ = job(pe, "norm", k)
                for e in range(2):
                    last = pe.matmul(b_[0:32, :], norm_sel[:, e, :], sq[:, (2 * k + e) % 4, :],
                                     start=(e == 0), stop=(e == 1))
                end(last)

            for i, (half, n, e) in enumerate(proj_order):
                b_ = job(pe, "proj", (half, n, e))
                src = lnTr if half else lnT
                for c in range(CC):
                    last = pe.matmul(b_, wT[:, c, half * D + e * P:half * D + (e + 1) * P],
                                     src[:, c, n * 512:(n + 1) * 512], start=(c == 0), stop=(c == CC - 1))
                end(last)
                if e == 1 and i > 1:
                    norm(i // 2 - 1)
            norm(7)
            for n in range(NT // 2):
                b_ = job(pe, "v", n)
                for i in range(2):
                    for c in range(CC):
                        last = pe.matmul(b_[:, i * D:(i + 1) * D], lnTr[:, c, (2 * n + i) * P:(2 * n + i + 1) * P],
                                         wT[:, c, 2 * D:3 * D], start=(c == 0), stop=(c == CC - 1), skip_group_check=True)
                end(last)

            def scores(it, g):
                gi = g % TILES
                u, jt = gi // TPB, key_tile[gi]
                if gi % TPB == 0:
                    pe.wait_ge(stack_in[u], it * (16 * (LOADS + 1)) + 16 * (LOADS + 1) * (1 + g // TILES))
                if slot_before(g) >= 0:
                    read_out(pe, it, slot_before(g))
                for q in range(2):
                    last = pe.matmul(ps[:, 2 * slot_of[gi] + q, :], st_k[0:STACK, u, jt * P:(jt + 1) * P],
                                     st_q[0:STACK, u, q * 512:(q + 1) * 512], start=True, stop=True)
                last.then_inc(qk_done, 1)

            def weighted(it, i):
                g = pv_pos[i]
                u, o = i // TPB, i // TPB % 2
                if i % TPB == 0:
                    pe.wait_ge(v_staged, it * UNITS + u + 1)
                    pe.wait_ge(finished, it * UNITS + u + 1)
                if is_factor(g):
                    pe.wait_ge(factor_done, it * FACTORS + g // HALF + 1)
                else:
                    pe.wait_ge(exp_done, it * ADDS + (g + 1 - factors_to(g)))
                for c in range(4):
                    last = pe.matmul(ps[32 * c:32 * c + 32, 6 + o, 0:D], v_st[:, u, key_tile[g], :],
                                     ring[:, g % TPB, c * D:(c + 1) * D],
                                     start=(i % TPB == 0), stop=(i % TPB == TPB - 1), skip_group_check=True)
                last.then_inc(pv_done, 1)

            def turn(wait, o):
                pe.wait_ge(heads_out, wait)
                for t in range(2):
                    last = pe.transpose(ps[:, 6 + o, D + t * P:D + (t + 1) * P], o_sb[:, o, t * P:(t + 1) * P], ident[:, :])
                last.then_inc(turned, 1)

            def attention(it, last=False):
                for i in range(TILES):
                    if i + AHEAD < TILES or not last:
                        scores(it, i + AHEAD)
                    weighted(it, i)
                    if i % TPB == TURN_AT:
                        turn(it * UNITS + (i // TPB + 1), (i // TPB + 1) % 2)

            taken(pe, index["v", NT // 2 - 1])
            for i in range(2):
                for t in range(2):
                    at = (1 - i) * D + t * P
                    last = pe.matmul(ps[:, 6 + i, at:at + P], ones[:, :], ones[:, :], start=True, stop=True,
                                     skip_group_check=True)
                last.then_inc(*((turned, 1), (pv_done, TPB))[i])
            pe.wait_ge(const_ready, 6)
            for g in range(AHEAD):
                scores(0, g)
            with pe.Fori(0, STEPS - 1) as it:
                attention(it)
            attention(STEPS - 1, last=True)
            turn(STEPS * UNITS + 1, 1)

            pe.wait_ge(worst_done, 1)
            pe.transpose(ps[0:1, 0, 0:P], worst[:, 0:1], ident[:, :]).then_inc(worst_turned, 1)
            pe.wait_ge(general_known, 1)
            with pe.If(pe.value_load(general[0:1, 0:1], min_val=0, max_val=1) > 0):
                pe.wait_ge(g_rows, 1)
                with pe.Fori(0, H) as h:
                    for b in range(B):
                        n = h * B + (b + 1)
                        base = h * (B * 2 * TPB) + b * 2 * TPB
                        pe.wait_ge(g_in, n * (16 * (LOADS + 1)))
                        for qt in range(TPB):
                            if qt >= 2:
                                pe.wait_ge(g_add, base + (qt - 1))
                            for q in range(2):
                                last = pe.matmul(ps[:, 2 * (qt % 2) + q, :], st_q[0:SHIFT_ROW, 0, qt * P:(qt + 1) * P],
                                                 st_k[0:SHIFT_ROW, 0, q * 512:(q + 1) * 512], start=True, stop=True)
                            last.then_inc(g_qk, 1)
                        pe.wait_ge(g_row, n * 16)
                        pe.wait_ge(g_v, n)
                        for jt in range(TPB):
                            pe.wait_ge(g_add, base + (TPB + jt - 1))
                            for q in range(2):
                                last = pe.matmul(ps[:, 2 * (jt % 2) + q, :], st_k[0:SHIFT_ROW + 2, 0, jt * P:(jt + 1) * P],
                                                 st_q[0:SHIFT_ROW + 2, 0, q * 512:(q + 1) * 512], start=True, stop=True)
                            last.then_inc(g_qk, 1)
                            pe.wait_ge(g_exp, h * (B * TPB) + (b * TPB + jt + 1))
                            for c in range(4):
                                last = pe.matmul(ps[32 * c:32 * c + 32, 6, 0:D], v_st[:, 0, jt, :],
                                                 ring[:, jt % 2, c * D:(c + 1) * D],
                                                 start=(jt == 0), stop=(jt == TPB - 1), skip_group_check=True)
                        last.then_inc(g_pv, 1)
                        pe.wait_ge(g_heads, n)
                        for t in range(2):
                            last = pe.transpose(ps[:, 6, D + t * P:D + (t + 1) * P], o_sb[:, 0, t * P:(t + 1) * P], ident[:, :])
                        last.then_inc(g_turned, 1)
                pe.wait_ge(g_fin, H * B + 1)

            for kind, k in plan:
                if kind == "wo":
                    for c in range(CC):
                        turn4("oT", (k, c), [(o_all[:, 4 * k + i, DH + c * P:DH + (c + 1) * P], ident, i * P) for i in range(4)])
                    taken(pe, index["oT", (k, 1)])
                    for n in range(2 * k, 2 * k + 2):
                        b_ = job(pe, "wo", n)
                        for i in range(2):
                            for c in range(CC):
                                last = pe.matmul(b_[:, i * D:(i + 1) * D], lnT[:, c, (2 * n + i) * P:(2 * n + i + 1) * P],
                                                 woT[:, c, :], start=(c == 0), stop=(c == CC - 1), skip_group_check=True)
                        end(last)
                elif kind in ("norm2T", "norm3T"):
                    turn_norm(kind, kind[:5], k, ident)
                elif kind == "logits":
                    taken(pe, index["norm2T", (k // 4, 1)])
                    for hf in range(2):
                        b_ = job(pe, "xl", (k, hf))
                        for c in range(CC):
                            last = pe.matmul(b_, lnT[:, c, k * P:(k + 1) * P],
                                             xa[:, c, k // TPB, hf * 512:(hf + 1) * 512], start=(c == 0), stop=(c == CC - 1))
                        end(last)
                elif kind == "probs":
                    pe.wait_ge(xprob_done, k + 1)
                    for hf in range(2):
                        turn4("xpT", (k, hf), [(xp[:, k % XBUF, hf * 512 + i * P:hf * 512 + (i + 1) * P], ident, i * P)
                                               for i in range(4)])
                elif kind == "out":
                    b_ = job(pe, "xo", k)
                    taken(pe, index["xpT", (k, 1)])
                    for i in range(NK):
                        last = pe.matmul(b_[:, 0:D], xpT[:, k % 3, i * P:(i + 1) * P], xvw[:, k // TPB, i, :],
                                         start=(i == 0), stop=(i == NK - 1))
                    end(last)
            taken(pe, index["norm3T", (3, 1)])
            pe.wait_ge(gate_in, 16)
            b_ = job(pe, "gate", 0)
            for c in range(CC):
                for n in range(4):
                    last = pe.matmul(b_[32 * n:32 * n + 32, :], gw_sb[:, c, :], lnT[:, c, n * 512:(n + 1) * 512],
                                     start=(c == 0), stop=(c == CC - 1), skip_group_check=True)
            end(last)
            taken(pe, index["gate", 0])
            turn4("gateT", 0, [(gT[:, i * P:(i + 1) * P], ident, i * P) for i in range(4)])

            def hidden(key):
                m, n = key
                b_ = job(pe, "w1", key)
                for c in range(CC):
                    last = pe.matmul(b_, w1[:, c, m * P:(m + 1) * P], lnT[:, c, n * 512:(n + 1) * 512],
                                     start=(c == 0), stop=(c == CC - 1))
                end(last)

            def second(t):
                b_ = job(pe, "w2", t)
                for m in range(NM):
                    pe.matmul(b_[:, 0:D], hid[:, m, t * P:(t + 1) * P], w2[:, m, :], start=(m == 0), stop=False)
                end(pe.matmul(b_[:, 0:D], sel_b[:, (t % TPB) * P:(t % TPB + 1) * P], b2p[:, t // TPB, :],
                              start=False, stop=True))

            pe.wait_ge(ffn_in, 16 * 9)
            for k in w1_order[:W1_EARLY]:
                hidden(k)
            pe.wait_ge(rrep_done, 1)
            for n in range(2):
                turn4("rrep", n, [(rrep[:, 4 * n + i, :], ident, i * P) for i in range(4)])
            for i in range(10):
                b_ = job(pe, "digit", i)
                pe.wait_ge(digit_asked, i + 1)
                end(pe.matmul(b_[:, 0:1], block8, r_s[:, 8:9].bitcast(BF16)[:, 0:1], start=True, stop=True))
                hidden(w1_order[W1_EARLY + i])
            for k in w1_order[W1_EARLY + 10:]:
                hidden(k)
            pe.wait_ge(chosen, 1)
            pe.wait_ge(b2_ready, 1)
            for n in range(4):
                for m in range(NM):
                    end(pe.matmul(job(pe, "mask", (m, n)), pick[:, (n // 2) * NM + m, :],
                                  sel_b[:, (n % 2) * 512:(n % 2 + 1) * 512], start=True, stop=True))
                if n:
                    taken(pe, index["mask", (NM - 1, n - 1)])
                    for t in range(4 * n - 4, 4 * n):
                        second(t)
            taken(pe, index["mask", (NM - 1, 3)])
            for t in range(12, NT):
                second(t)

        @block.vector
        def _(dve):
            step = Counter(dve, dve_step)

            def layer_norm(kind, g):
                i_ = ln_order.index((kind, g))
                for i in range(3 if (kind, g) == ("norm3", 3) else 0, 4):
                    dve.bn_stats(st[:, i, :], xt[:, 4 * g + i, :]).then_inc(dve_step, 1)
                    step.n += 1
                dve.wait_ge(dve_step, step.n)
                for i in range(4):
                    dve.bn_aggr(mv[:, i, :], st[:, i, :]).then_inc(dve_step, 1)
                step.n += 4
                dve.wait_ge(dve_step, step.n)
                var, r_, a_, b_ = (ln_s[:, i, :] for i in range(4))
                step(dve.tensor_scalar(var, mv[:, :, 1], LN_EPS, None, ALU.add))
                step(dve.tensor_scalar(a_.bitcast(I32), var.bitcast(I32), 1, None, ALU.logical_shift_right))
                step(dve.tensor_scalar(r_.bitcast(I32), a_.bitcast(I32), -1.0, float(0x5F3759DF), ALU.mult, ALU.add))
                for _ in range(3):
                    step(dve.tensor_tensor(a_, r_, r_, ALU.mult))
                    step(dve.scalar_tensor_tensor(out=b_, in0=a_, scalar=-0.5, in1=var, op0=ALU.mult, op1=ALU.mult))
                    step(dve.scalar_tensor_tensor(out=r_, in0=b_, scalar=1.5, in1=r_, op0=ALU.add, op1=ALU.mult))
                if i_ >= 2:
                    before, g_ = ln_order[i_ - 2]
                    after(dve, "lnTr" if before == "norm1" else before + "T", (g_, 1))
                for i in range(4):
                    ins = dve.tensor_scalar(xn[:, i_ % 2, i, :], xt[:, 4 * g + i, :], mv[:, i, 0:1], r_[:, i:i + 1],
                                            ALU.subtract, ALU.mult)
                    if i == 3:
                        ins.then_inc(ln_done, 1)
                dve.wait_ge(ln_done, i_ + 1)

            def first_norm(g):
                dve.wait_ge(x_in[g], 16)
                layer_norm("norm1", g)

            def context_values(n):
                b_ = result(dve, "vT", n)
                for hl in range(2):
                    rows = slice(64 * hl, 64 * hl + 64)
                    ins = dve.tensor_copy(
                        vbd.rearrange("p (b k) c -> p b k c", b=B)[rows, :, 4 * n:4 * n + 4, 64 * hl:64 * hl + 64],
                        b_[rows, :].rearrange("p (k b c) -> p b k c", k=4, b=B))
                ins.then_inc(dve_took, 1)

            first_norm(0)
            first_norm(1)
            dve.tensor_copy(ceff, result(dve, "ceff", 0)[0:TAPS, 0:H]).then_inc(dve_took, 1)
            b_ = result(dve, "bias", 0)[0:H, 0:RES]
            step(dve.tensor_reduce(head_s[:, 6:7], b_, AX.X, ALU.max))
            dve.tensor_scalar(bias_h, b_, head_s[:, 6:7], None, ALU.subtract).then_inc(dve_took, 1)
            dve.wait_ge(const_ready, 4)
            dve.tensor_copy(biasT[:, 0:H], result(dve, "biasT", 0)[:, 0:H]).then_inc(dve_took, 1)
            first_norm(2)
            context_values(0)
            dve.tensor_copy(line_sb, result(dve, "line", 0)).then_inc(dve_took, 1)
            context_values(1)
            first_norm(3)
            xvw_2 = xvw_f.rearrange("p (n c) -> p n c", n=8)
            for n in range(8):
                dve.tensor_copy(xvw_2[:, n, :], result(dve, "xvw", n)).then_inc(dve_took, 1)

            for i, (half, n, e) in enumerate(proj_order):
                dve.wait_ge(part1_done, i + 1)
                if i >= 4:
                    dve.wait_ge(part3_done, i - 3)
                p1 = parts[half][:, e, 0, n * 512:(n + 1) * 512]
                dve.scalar_tensor_tensor(out=resid[:, i % 4, :], in0=bank(index["proj", (half, n, e)]),
                                         scalar=SCALE if half == 0 else 1.0, in1=p1, op0=ALU.mult,
                                         op1=ALU.subtract).then_inc(dve_took, 1)
                if i >= 4:
                    after(dve, "norm", i // 2 - 2)
                dve.tensor_tensor(sq[:, i % 4, :], p1, p1, ALU.mult).then_inc(sq_done, 1)
                k = i // 2 - 1
                if e == 1 and 0 <= k < 4:
                    dve.tensor_reduce(head_s[:, k:k + 1], result(dve, "norm", k)[0:H, :], AX.X, ALU.max).then_inc(dve_took, 1)
                    if k == 3:
                        taken(dve, index["norm", 3])
                        step(dve.tensor_reduce(head_s[:, 4:6], head_s[:, 0:4].rearrange("p (b n) -> p b n", b=B), AX.X, ALU.max))
                        dve.tensor_scalar(head_s[:, 4:6], head_s[:, 4:6], UMARGIN, None, ALU.mult).then_inc(kmax_done, 1)

            def take_sums(n, b):
                heads = ps[:, 6 + b, D:2 * D].rearrange("p (t c d) -> p t c d", t=2, c=4)
                dve.wait_ge(turned, n + 1)
                dve.tensor_scalar(sums_[:, :, :], heads[:, :, :, DH], LEAST_SUM, None, ALU.max).then_inc(attn_step, 1)

            def finish(col, n, b):
                heads = ps[:, 6 + b, D:2 * D].rearrange("p (t c d) -> p t c d", t=2, c=4)
                dve.wait_ge(attn_step, n * 3 + 1)
                dve.reciprocal(rs[:, :, :], sums_[:, :, :]).then_inc(attn_step, 1)
                dve.tensor_tensor(low[:, :, :], low[:, :, :], sums_[:, :, :], ALU.min).then_inc(attn_step, 1)
                dve.wait_ge(attn_step, n * 3 + 2)
                dst = o_all[:, b * TPB:(b + 1) * TPB, :].rearrange("p (c t) k -> p t c k", t=2)[:, :, :, bass.ds(col, DH)]
                dve.tensor_tensor(dst, heads[:, :, :, 0:DH], rs[:, :, :].unsqueeze(3).broadcast_to([P, 2, 4, DH]),
                                  ALU.mult).then_inc(finished, 1)
                dve.wait_ge(attn_step, n * 3 + 3)

            step(dve.memset(low[:, :, :], 1.0))
            with dve.Fori(0, STEPS) as it:
                for g in range(TILES):
                    if is_factor(g):
                        continue
                    u, jt = g // TPB, key_tile[g]
                    if g % (2 * TPB) == 0:
                        dve.wait_ge(slab_in[u // 2], it * 16 + 16)
                    dve.wait_ge(qk_done, it * TILES + g + 1)
                    ring_free(dve, it, g)
                    at = (jt - FACTOR_TILES) * P
                    dve.tensor_tensor(ring[:, g % TPB, :],
                                      ps[:, 2 * slot_of[g]:2 * slot_of[g] + 2, :].rearrange("p a b -> p (a b)"),
                                      slab[:, u // 2, at:at + S], ALU.add).then_inc(add_done, 1)
                    if g % TPB == SUMS_AT:
                        take_sums(it * UNITS + u, u % 2)
                    if g % TPB == FIN_AT:
                        finish((it * 2 + u // 2) * DH, it * UNITS + u, u % 2)
            for b in range(B):
                dve.wait_ge(finished, STEPS * UNITS + b)
                take_sums(STEPS * UNITS + b, b)
                finish(H * DH, STEPS * UNITS + b, b)
            dve.wait_ge(finished, STEPS * UNITS + B)

            step(dve.tensor_reduce(worst[:, 0:1], low[:, :, :].rearrange("p a b -> p (a b)"), AX.X, ALU.min))
            dve.sem_inc(worst_done, 1)
            dve.wait_ge(worst_turned, 1)
            step(dve.tensor_reduce(worst[0:1, 1:2], ps[0:1, 0, 0:P], AX.X, ALU.min))
            dve.tensor_scalar(general[:, :], worst[0:1, 1:2], LOW_SUM, None, ALU.is_lt).then_inc(general_known, 1)
            dve.wait_ge(general_known, 1)
            with dve.If(dve.value_load(general[0:1, 0:1], min_val=0, max_val=1) > 0):
                dve.sem_inc(g_fin, 1)
                with dve.Fori(0, H) as h:
                    for b in range(B):
                        n = h * B + (b + 1)
                        base = h * (B * 2 * TPB) + b * 2 * TPB
                        s0 = h * (B * (TPB + 4)) + b * (TPB + 4)
                        for qt in range(TPB):
                            dve.wait_ge(g_qk, base + (qt + 1))
                            if qt:
                                dve.wait_ge(g_step, s0 + qt)
                            dve.tensor_tensor(ring[:, qt % 2, :],
                                              ps[:, 2 * (qt % 2):2 * (qt % 2) + 2, :].rearrange("p a b -> p (a b)"),
                                              slab_g[:, qt * P:qt * P + S], ALU.add).then_inc(g_add, 1)
                            dve.wait_ge(g_add, base + (qt + 1))
                            dve.tensor_reduce(mx[:, qt:qt + 1], ring[:, qt % 2, :], AX.X, ALU.max).then_inc(g_step, 1)
                        dve.wait_ge(g_step, s0 + TPB)
                        dve.tensor_copy(mx_p[:, 0, :], mx[:, :]).then_inc(g_step, 1)
                        dve.wait_ge(g_step, s0 + (TPB + 1))
                        dve.tensor_tensor(mx[:, :], mx[:, :], mx_p[:, 0, :], ALU.subtract).then_inc(g_step, 1)
                        dve.wait_ge(g_step, s0 + (TPB + 2))
                        dve.tensor_copy(mx_p[:, 1, :], mx[:, :]).then_inc(g_max, 1)
                        for jt in range(TPB):
                            dve.wait_ge(g_qk, base + (TPB + jt + 1))
                            dve.tensor_tensor(ring[:, jt % 2, :],
                                              ps[:, 2 * (jt % 2):2 * (jt % 2) + 2, :].rearrange("p a b -> p (a b)"),
                                              slab_g[:, jt * P:jt * P + S], ALU.add).then_inc(g_add, 1)
                        heads = ps[:, 6, D:2 * D].rearrange("p (t c d) -> p t c d", t=2, c=4)
                        dve.wait_ge(g_turned, n)
                        dve.reciprocal(rs[:, :, :], heads[:, :, :, DH]).then_inc(g_step, 1)
                        dve.wait_ge(g_step, s0 + (TPB + 3))
                        dst = o_all[:, b * TPB:(b + 1) * TPB, :].rearrange("p (c t) k -> p t c k", t=2)[
                            :, :, :, bass.ds(h * DH + DH, DH)]
                        dve.tensor_tensor(dst, heads[:, :, :, 0:DH], rs[:, :, :].unsqueeze(3).broadcast_to([P, 2, 4, DH]),
                                          ALU.mult).then_inc(g_fin, 1)
                        dve.wait_ge(g_fin, n + 1)
                        dve.sem_inc(g_step, 1)

            def sums(t):
                dve.wait_ge(xexp_done, t + 1)
                step(dve.tensor_reduce(x_s[:, 1, t % 8, :], xp[:, t % XBUF, :].rearrange("p (h k) -> p h k", k=KV),
                                       AX.X, ALU.add))
                dve.reciprocal(x_s[:, 1, t % 8, :], x_s[:, 1, t % 8, :]).then_inc(xrecip_done, 1)

            def finish_tile(t):
                if t >= 4:
                    dve.wait_ge(stored[t % 4], 16 * (t // 4))
                dve.tensor_tensor(o_out[:, t % 4, 0:D], result(dve, "w2", t)[:, 0:D], xt[:, t, :], ALU.add).then_inc(out_done, 1)
                dve.wait_ge(out_done, t + 1)
                dve.sem_inc(dve_took, 1)

            dve.wait_ge(ffn_const, 1)
            for kind, k in plan:
                if kind == "wo":
                    for n in range(2 * k, 2 * k + 2):
                        dve.tensor_tensor(xt[:, 2 * n:2 * n + 2, :].rearrange("p a b -> p (a b)"), result(dve, "wo", n),
                                          xt[:, 2 * n:2 * n + 2, :].rearrange("p a b -> p (a b)"), ALU.add).then_inc(dve_took, 1)
                elif kind == "norm2":
                    taken(dve, index["wo", 2 * k + 1])
                    layer_norm(kind, k)
                elif kind == "norm3":
                    taken(dve, index["xo", 4 * k + 3])
                    layer_norm(kind, k)
                elif kind == "logits":
                    if k >= XBUF:
                        after(dve, "xpT", (k - XBUF, 1))
                    for hf in range(2):
                        b_ = result(dve, "xl", (k, hf)).rearrange("p (h k) -> p h k", k=KV)
                        m = x_s[:, 0, k % 8, 8 * hf:8 * hf + 8]
                        step(dve.tensor_reduce(m, b_, AX.X, ALU.max))
                        dve.tensor_tensor(xp[:, k % XBUF, hf * 512:(hf + 1) * 512].rearrange("p (h k) -> p h k", k=KV), b_,
                                          m.unsqueeze(2).broadcast_to([P, 8, KV]), ALU.subtract).then_inc(centred, 1)
                        dve.wait_ge(centred, 2 * k + hf + 1)
                        dve.sem_inc(dve_took, 1)
                    if k:
                        sums(k - 1)
                elif kind == "probs":
                    if k == NT - TURN_LAG:
                        sums(NT - 1)
                elif kind == "out":
                    if k % 4 == 0:
                        dve.wait_ge(bo_added, k // 4 + 1)
                    dve.tensor_tensor(xt[:, k, :], result(dve, "xo", k)[:, 0:D], xt[:, k, :], ALU.add).then_inc(dve_took, 1)
                    if NT - 4 <= k < NT - 1:
                        taken(dve, index["xo", k])
                        step(dve.bn_stats(st[:, k % 4, :], xt[:, k, :]))

            lane = r_s[:, 12:13].bitcast(I32)
            step(dve.tensor_scalar(lane, lane, 7, None, ALU.bitwise_and))
            for i in range(10):
                step(dve.tensor_scalar(digits[:, i:i + 1].bitcast(I32), lane, 27 - 3 * i, None, ALU.logical_shift_left))
            thr, cand, count, ask, got = (r_s[:, i:i + 1] for i in (1, 2, 3, 8, 5))
            step(dve.memset(thr, 0.0))
            g_ = [gates[:, i, :].rearrange("p (t e) -> p t e", e=E) for i in range(4)]
            m16_ = m16[:, :]
            wb = expw.unsqueeze(1).broadcast_to([P, NT, E])

            def wide(v):
                return v.unsqueeze(2).broadcast_to([P, NT, E])

            step(dve.tensor_tensor(gates[:, 2, :].rearrange("p (n q e) -> p n q e", n=4, e=E),
                                   result(dve, "gateT", 0).rearrange("p (q n e) -> p n q e", n=4, e=32)[:, :, :, 0:E],
                                   gb_bc[:, :].unsqueeze(1).unsqueeze(1).broadcast_to([P, 4, 4, E]), ALU.add))
            dve.sem_inc(dve_took, 1)
            step(dve.tensor_reduce(m16_, g_[2], AX.X, ALU.max))
            dve.tensor_tensor(g_[0], g_[2], wide(m16_), ALU.subtract).then_inc(gcentred, 1)
            dve.wait_ge(gexp_done, 1)
            step(dve.tensor_reduce(m16_, g_[1], AX.X, ALU.add))
            step(dve.reciprocal(m16_, m16_))
            step(dve.tensor_tensor(g_[1], g_[1], wide(m16_), ALU.mult))
            for k, (values, chosen_) in enumerate(((g_[1], g_[3]), (g_[0], g_[2]))):
                step(dve.tensor_reduce(m16_, values, AX.X, ALU.max))
                step(dve.tensor_tensor(g_[2], values, wide(m16_), ALU.is_equal))
                step(dve.tensor_tensor(g_[2], g_[2], wb, ALU.mult))
                step(dve.tensor_reduce(m16_, g_[2], AX.X, ALU.max))
                step(dve.tensor_tensor(chosen_, wide(m16_), wb, ALU.is_equal))
                if k == 0:
                    step(dve.scalar_tensor_tensor(out=gates[:, 0, :], in0=gates[:, 3, :], scalar=-2.0, in1=gates[:, 1, :],
                                                  op0=ALU.mult, op1=ALU.add))
            step(dve.tensor_tensor(g_[3], g_[3], g_[2], ALU.add))
            step(dve.tensor_tensor(g_[1], g_[1], g_[3], ALU.mult))
            half = NT * E // B
            step(dve.tensor_tensor(gates[:, 0, 0:half], gates[:, 1, 0:half], gates[:, 1, half:2 * half], ALU.add))
            step(dve.tensor_scalar(gates[:, 0, 0:half], gates[:, 0, 0:half], DEN_EPS, None, ALU.add))
            step(dve.reciprocal(gates[:, 0, 0:half], gates[:, 0, 0:half]))
            for b in range(B):
                step(dve.tensor_tensor(gates[:, 2, b * half:(b + 1) * half], gates[:, 1, b * half:(b + 1) * half],
                                       gates[:, 0, 0:half], ALU.mult))
            for b in range(B):
                v = g_[2][:, b * TPB:(b + 1) * TPB, :].unsqueeze(3).broadcast_to([P, TPB, E, 8])
                step(dve.tensor_copy(rrep[:, :, b * 64:(b + 1) * 64].rearrange("p t (e c) -> p t e c", c=8), v))
            dve.sem_inc(rrep_done, 1)
            dve.tensor_copy(rr[:, 0:512], result(dve, "rrep", 0)).then_inc(dve_took, 1)
            taken(dve, index["rrep", 0])
            taken(dve, index["rrep", 1])
            for i in range(10):
                step(dve.tensor_tensor(cand.bitcast(U32), thr.bitcast(U32), digits[:, i:i + 1], ALU.bitwise_or))
                step(dve.tensor_scalar(junk, rr, cand, None, ALU.is_ge, ALU.add, accum_out=count))
                dve.tensor_scalar(ask.bitcast(BF16)[:, 0:1], count, float(KSEL), None, ALU.is_ge).then_inc(digit_asked, 1)
                b_ = result(dve, "digit", i)
                step(dve.tensor_scalar(got.bitcast(U32), b_[:, 0:1], -1.0, float(1 << (27 - 3 * i)), ALU.add, ALU.mult))
                dve.sem_inc(dve_took, 1)
                step(dve.tensor_tensor(thr.bitcast(U32), thr.bitcast(U32), got.bitcast(U32), ALU.bitwise_or))
            step(dve.tensor_scalar(above, rr, thr, None, ALU.is_gt, ALU.add, accum_out=count))
            step(dve.tensor_scalar(count, count, -1.0, float(KSEL), ALU.mult, ALU.add))
            step(dve.tensor_scalar(rr, rr, thr, None, ALU.is_equal))
            step(dve.tensor_tensor_scan(prefix, rr, rr, 0.0, ALU.add, ALU.bypass))
            step(dve.scalar_tensor_tensor(out=prefix, in0=prefix, scalar=count, in1=rr, op0=ALU.is_le, op1=ALU.mult))
            dve.tensor_tensor(sel_b, above, prefix, ALU.add).then_inc(chosen, 1)

            for n in range(4):
                for m in range(NM):
                    taken(dve, index["w1", (m, n)])
                    h_ = hid[:, m, n * 512:(n + 1) * 512]
                    dve.tensor_tensor(h_, result(dve, "mask", (m, n)), h_, ALU.mult).then_inc(dve_took, 1)
                for t in (range(4 * n - 4, 4 * n) if n else ()):
                    finish_tile(t)
            for t in range(12, NT):
                finish_tile(t)


_INS = ["x", "ctx_768", "L0_attn_Wqkv", "L0_attn_Wout", "L0_attn_Wpos", "L0_attn_coeffs", "L0_xattn_w_q",
        "L0_xattn_w_k", "L0_xattn_w_v", "L0_xattn_w_out", "L0_xattn_b_out", "L0_ffn_w_gate_w", "L0_ffn_w_gate_b",
        "L0_ffn_W1", "L0_ffn_b1", "L0_ffn_W2", "L0_ffn_b2"]
_OUTS = [((B, S, D), "float32")]


def kernel(**inputs):
    import numpy as _np
    import concourse.bacc as _bacc
    from concourse import mybir as _mybir
    from concourse.bass_utils import run_bass_kernel_spmd as _run

    nc = _bacc.Bacc("TRN2", target_bir_lowering=False, num_devices=1)
    arrays, args = {}, []
    for name in _INS:
        a = _np.ascontiguousarray(inputs[name])
        arrays[f"in_{name}_dram"] = a
        args.append(nc.dram_tensor(f"in_{name}_dram", a.shape, _mybir.dt.from_np(a.dtype), kind="ExternalInput").ap())
    for i, (shape, dtype) in enumerate(_OUTS):
        dt = _mybir.dt.from_np(_np.dtype(dtype))
        args.append(nc.dram_tensor(f"out_{i}_dram", shape, dt, kind="ExternalOutput").ap())
    decoder_layer(nc, *args)
    r = _run(nc, [arrays], core_ids=[0])
    got = tuple(r.results[0][f"out_{i}_dram"] for i in range(len(_OUTS)))
    return got[0]
```
